# Optimizing a Trainium2 kernel written in Bass

```python
import numpy as np
import jax
import jax.numpy as jnp

def _softmax(x, axis=-1):
    return jax.nn.softmax(x, axis=axis)

def _gelu(x):
    return jax.nn.gelu(x, approximate=True)

def _silu(x):
    return jax.nn.silu(x)

def _sigmoid(x):
    return jax.nn.sigmoid(x)

def _layernorm(x, axis=-1, eps=1e-05):
    m = jnp.mean(x, axis=axis, keepdims=True)
    v = jnp.var(x, axis=axis, keepdims=True)
    return (x - m) / jnp.sqrt(v + eps)

def _scatter_add(tgt, idx, src, axis=0):
    return tgt.at[idx].add(src)

def _segment_sum(src, seg, n):
    return jax.ops.segment_sum(src, seg, n)
kernel_name = 'mk_xattn_ffn_d1_seqx_r4_0a30d2'

def setup_inputs(seed: int=0):
    np.random.seed(seed)
    _w = jnp.asarray

    def _rec_inputs():
        import jax
        import jax.numpy as jnp
        _rk = jax.random.key(seed)
        x = -0.0003929 + 0.9999 * jax.random.normal(jax.random.fold_in(_rk, 1), (128, 128, 256), jnp.float32)
        _lenS = 128 - jax.random.randint(jax.random.fold_in(_rk, 7), (128,), 0, max(1, 128 // 4) + 1, jnp.int32)
        _lenS2 = 128 - jax.random.randint(jax.random.fold_in(_rk, 8), (128,), 0, max(1, 128 // 4) + 1, jnp.int32)
        _ctx_1024P = jax.random.normal(jax.random.fold_in(_rk, 11), (128, 16, 256), jnp.float32)
        _ctx_1024c = jax.random.dirichlet(jax.random.fold_in(_rk, 511), 0.3 * jnp.ones((16,), jnp.float32), (128, 128))
        _ctx_1024t = jnp.einsum('bsk,bkd->bsd', _ctx_1024c, _ctx_1024P)
        _ctx_1024t = _ctx_1024t * jax.lax.rsqrt(jnp.mean(jnp.square(_ctx_1024t)) + 1e-12) * 0.953939
        ctx_1024 = 2.81802e-05 + 1.00001 * (_ctx_1024t + 0.3 * jax.random.normal(jax.random.fold_in(_rk, 611), (128, 128, 256), jnp.float32))
        return (x, ctx_1024)
    x, ctx_1024 = _rec_inputs()

    def _L0_xattn_setup():
        import jax, jax.numpy as jnp
        import numpy as np
        import math
        D_MODEL = 256
        N_HEADS = 16
        C = 1
        B, L = (8, 512)

        def _glorot(key, fan):
            lim = np.sqrt(6.0 / (fan + fan)).astype(np.float32)
            return jax.random.uniform(key, (fan, fan), jnp.float32, -lim, lim)
        key = jax.random.key(seed)
        ks = jax.random.split(key, 7)
        queries = jax.random.normal(ks[0], (B, L, D_MODEL), jnp.float32)
        keys = jax.random.normal(ks[1], (B, L, D_MODEL), jnp.float32)
        values = jax.random.normal(ks[2], (B, L, D_MODEL), jnp.float32)
        wq = _glorot(ks[3], D_MODEL)
        wk = _glorot(ks[4], D_MODEL)
        wv = _glorot(ks[5], D_MODEL)
        wo = _glorot(ks[6], D_MODEL)
        return {'queries': queries, 'keys': keys, 'values': values, 'wq': wq, 'wk': wk, 'wv': wv, 'wo': wo}
    _L0_xattn_all = _L0_xattn_setup()
    _L0_xattn_in = {k: v for k, v in _L0_xattn_all.items() if k in ('wq', 'wk', 'wv', 'wo')}
    del _L0_xattn_all

    def _L0_ffn_setup():
        import jax, jax.numpy as jnp
        import numpy as np

        def _ste(w, w_q):
            return w + jax.lax.stop_gradient(w_q - w)

        def quantize_w8_per(w, axis):
            amax = jnp.clip(jnp.max(jnp.abs(w), axis=axis, keepdims=True), 1e-08, None)
            scale = 127.0 / amax
            w_q = jnp.clip(jnp.round(w * scale), -128.0, 127.0) / scale
            return _ste(w, w_q)

        def quantize_a16(x):
            amax = jnp.clip(jnp.max(jnp.abs(x)), 1e-08, None)
            scale = 32767.0 / amax
            x_q = jnp.clip(jnp.round(x * scale), -32768.0, 32767.0) / scale
            return _ste(x, x_q)
        key = jax.random.key(seed)
        k1, k2, k3 = jax.random.split(key, 3)
        d_model, d_ff = (256, 1024)
        x = jax.random.normal(k1, (4, 512, d_model), dtype=jnp.float32)
        W_in = jax.random.normal(k2, (d_model, d_ff), dtype=jnp.float32) / np.sqrt(d_model)
        b_in = jnp.zeros((d_ff,), dtype=jnp.float32)
        W_out = jax.random.normal(k3, (d_ff, d_model), dtype=jnp.float32) / np.sqrt(d_ff)
        b_out = jnp.zeros((d_model,), dtype=jnp.float32)
        return {'x': x, 'W_in': W_in, 'b_in': b_in, 'W_out': W_out, 'b_out': b_out}
    _L0_ffn_all = _L0_ffn_setup()
    _L0_ffn_in = {k: v for k, v in _L0_ffn_all.items() if k in ('W_in', 'b_in', 'W_out', 'b_out')}
    del _L0_ffn_all
    return {'x': x, 'ctx_1024': ctx_1024, 'L0_xattn_wq': _L0_xattn_in['wq'], 'L0_xattn_wk': _L0_xattn_in['wk'], 'L0_xattn_wv': _L0_xattn_in['wv'], 'L0_xattn_wo': _L0_xattn_in['wo'], 'L0_ffn_W_in': _L0_ffn_in['W_in'], 'L0_ffn_b_in': _L0_ffn_in['b_in'], 'L0_ffn_W_out': _L0_ffn_in['W_out'], 'L0_ffn_b_out': _L0_ffn_in['b_out']}

def reference(x, ctx_1024, L0_xattn_wq, L0_xattn_wk, L0_xattn_wv, L0_xattn_wo, L0_ffn_W_in, L0_ffn_b_in, L0_ffn_W_out, L0_ffn_b_out):
    import jax
    import jax.numpy as jnp

    def _L0_xattn_ref(queries, keys, values, wq, wk, wv, wo):
        import jax, jax.numpy as jnp
        import numpy as np
        import math
        D_MODEL = 256
        N_HEADS = 16
        C = 1
        B, L = (8, 512)

        def _glorot(key, fan):
            lim = np.sqrt(6.0 / (fan + fan)).astype(np.float32)
            return jax.random.uniform(key, (fan, fan), jnp.float32, -lim, lim)
        Bv, Lv, _ = queries.shape
        H = N_HEADS
        Dh = D_MODEL // N_HEADS
        Q = (queries @ wq).reshape(Bv, Lv, H, Dh).transpose(0, 2, 3, 1)
        K = (keys @ wk).reshape(Bv, Lv, H, Dh).transpose(0, 2, 3, 1)
        V = (values @ wv).reshape(Bv, Lv, H, Dh).transpose(0, 2, 3, 1)
        corr = jnp.fft.irfft(jnp.fft.rfft(Q, axis=-1) * jnp.conj(jnp.fft.rfft(K, axis=-1)), n=Lv, axis=-1)
        k_top = int(math.floor(C * math.log(Lv)))
        top_vals, top_idx = jax.lax.top_k(corr, k_top)
        w = jax.nn.softmax(top_vals, axis=-1)
        t = jnp.arange(Dh)
        out = jnp.zeros_like(V)
        for i in range(k_top):
            gather_idx = (t[None, None, :] - top_idx[..., i]) % Dh
            rolled = jnp.take_along_axis(V, gather_idx[..., None], axis=2)
            out = out + w[..., i, None] * rolled
        out = out.transpose(0, 2, 1, 3).reshape(Bv, Lv, D_MODEL)
        return out @ wo

    def _L0_ffn_ref(x, W_in, b_in, W_out, b_out):
        import jax, jax.numpy as jnp
        import numpy as np

        def _ste(w, w_q):
            return w + jax.lax.stop_gradient(w_q - w)

        def quantize_w8_per(w, axis):
            amax = jnp.clip(jnp.max(jnp.abs(w), axis=axis, keepdims=True), 1e-08, None)
            scale = 127.0 / amax
            w_q = jnp.clip(jnp.round(w * scale), -128.0, 127.0) / scale
            return _ste(w, w_q)

        def quantize_a16(x):
            amax = jnp.clip(jnp.max(jnp.abs(x)), 1e-08, None)
            scale = 32767.0 / amax
            x_q = jnp.clip(jnp.round(x * scale), -32768.0, 32767.0) / scale
            return _ste(x, x_q)
        W_in_sim = quantize_w8_per(W_in, axis=0)
        W_out_sim = quantize_w8_per(W_out, axis=1)
        x_sim = quantize_a16(x)
        hidden = jax.nn.gelu(x_sim @ W_in_sim + b_in, approximate=False)
        hidden_sim = quantize_a16(hidden)
        out = hidden_sim @ W_out_sim + b_out
        return out
    x = x + _L0_xattn_ref(_layernorm(x, axis=-1), ctx_1024, ctx_1024, L0_xattn_wq, L0_xattn_wk, L0_xattn_wv, L0_xattn_wo)
    x = x + _L0_ffn_ref(_layernorm(x, axis=-1), L0_ffn_W_in, L0_ffn_b_in, L0_ffn_W_out, L0_ffn_b_out)
    return x

_drawn_inputs = setup_inputs


def setup_inputs(seed=0):
    import zlib

    import numpy as np

    out = dict(_drawn_inputs(seed))
    spreads = {'L0_ffn_b_in': (0.0, 0.1), 'L0_ffn_b_out': (0.0, 0.1)}
    factors = {}
    for name, (base, spread) in spreads.items():
        noise = np.random.default_rng([zlib.crc32(name.encode()), seed]).standard_normal(out[name].shape)
        drawn = base * np.exp(spread * noise) if base else spread * noise
        out[name] = jnp.asarray(drawn.astype(out[name].dtype))
    for name, factor in factors.items():
        out[name] = (out[name] * factor).astype(out[name].dtype)
    return out
```

```python
from contextlib import ExitStack

import concourse.bass as bass
from concourse import mybir

ALU = mybir.AluOpType
ACT = mybir.ActivationFunctionType
F32 = mybir.dt.float32
F16 = mybir.dt.float16
I16 = mybir.dt.int16
I32 = mybir.dt.int32
U32 = mybir.dt.uint32
AX_X = mybir.AxisListType.X
AX_XY = mybir.AxisListType.XY
RMAX = bass.bass_isa.ReduceOp.max

P = 128
HD = 16
NH = P // HD
NF = P // 2
KTOP = 4
UNROLL = 4
LAST = 3
INT16 = 32767.0
INT8 = 127.0
TINY = 1e-8
EPS = 1e-5

C_DFT = 0
C_INV = C_DFT + P
C_ID = C_INV + 4 * 2 * P
C_MASK = C_ID + P
C_IOTA = C_MASK + P
C_LOW = C_IOTA + HD
C_ALL = C_LOW + 1


def constants():
    import numpy as np
    t = np.arange(P)
    f = np.arange(NF)
    table = np.zeros((P, C_ALL), np.float64)
    angle = 2 * np.pi * np.outer(t, f) / P
    table[:, C_DFT:C_DFT + NF] = np.cos(angle)
    table[:, C_DFT + NF:C_DFT + P] = -np.sin(angle)
    table[:, C_DFT + NF] = np.cos(np.pi * t)
    cos = 2 * np.cos(angle.T) / P
    sin = 2 * np.sin(angle.T) / P
    cos_rr, cos_ii = cos.copy(), cos.copy()
    cos_rr[0] = 1.0 / P
    cos_ii[0] = np.cos(np.pi * t) / P
    for n, m in enumerate((cos_rr, cos_ii, -sin, sin)):
        at = C_INV + n * 2 * P
        for b in range(2):
            table[b * NF:(b + 1) * NF, at + b * P:at + (b + 1) * P] = m
    table[:, C_ID:C_ID + P] = np.eye(P)
    table[:, C_MASK:C_MASK + P] = (t[:, None] % NH) == (t[None, :] % NH)
    table[:, C_IOTA:C_IOTA + HD] = np.arange(HD)
    table[:, C_LOW] = t // NH + P
    return table.astype(np.float32)


def xattn_ffn_kernel(nc, x, ctx_in, wq, wk, wv, wo, w_in, b_in, w_out, b_out, table, out, x1_dram):
    B, L, D = x.shape
    FF = w_in.shape[1]
    DC = D // P
    FC = FF // P
    PAIRS = B // 2
    QUADS = B // 4
    assert L == P and DC == 2 and (PAIRS - UNROLL) % UNROLL == 0 and QUADS % 2 == 0

    x_v = x.rearrange("(n b) l d -> n l b d", b=2)
    c_v = ctx_in.rearrange("(n b) l d -> n l b d", b=2)
    x1_v = x1_dram.rearrange("(n b) l d -> n l b d", b=2)
    x1_q = x1_dram.rearrange("(n b) l d -> n l b d", b=4)
    out_q = out.rearrange("(n b) l d -> n l b d", b=4)

    with ExitStack() as ctx:
        def sb(name, shape, dt):
            return ctx.enter_context(nc.sbuf_tensor(name, shape, dt))

        def sem(name):
            return ctx.enter_context(nc.semaphore(name))

        cst = sb("cst", [P, C_ALL], F32)
        dft = cst[:, C_DFT:C_DFT + P]
        ident = cst[:, C_ID:C_ID + P]
        mask = cst[:, C_MASK:C_MASK + P]
        low = cst[:, C_LOW:C_LOW + 1]
        w_attn = sb("w_attn", [P, 4, DC, D], F32)
        win16 = sb("win16", [P, DC, FF], F16)
        wout16 = sb("wout16", [P, FC, D], F16)
        xnt = sb("xnt", [P, PAIRS, DC, 2, P], F32)
        xq = xnt[:, :, :, :, :].bitcast(F16).rearrange("p n c b l -> p (n c b l)").rearrange(
            "p (q s c t) -> p q s c t", q=QUADS, s=2, c=DC)
        b_in_sb = sb("b_in_sb", [P, FC], F32)
        b_out_sb = sb("b_out_sb", [P, D], F32)
        xmax = sb("xmax", [P, PAIRS], F32)
        hmax = sb("hmax", [P, QUADS, FC], F32)
        win_max = sb("win_max", [P, FC], F32)
        win_up = sb("win_up", [P, FC], F32)
        wout_max = sb("wout_max", [P, FC], F32)
        wout_up = sb("wout_up", [P, FC], F32)
        wout_rel = sb("wout_rel", [P, FC], F32)
        z_scale = sb("z_scale", [P, FC], F32)
        one = sb("one", [P, 12], F32)
        x_amax, x_up, h_amax, h_up, y_scale, wo_top, wo_topr, wo_part, xm_part, hm_part = [
            one[:, n:n + 1] for n in range(10)]

        ARENA = 13312
        arena = sb("arena", [P, ARENA], F32)
        at = [0]

        def cut(n, words, shape):
            a = at[0]
            at[0] += n * words
            assert at[0] <= ARENA
            return [arena[:, a + k * words:a + (k + 1) * words].rearrange(shape[0], **shape[1]) for k in range(n)]

        PAIR = ("p (b d) -> p b d", dict(b=2))
        FOUR = ("p (c b l) -> p c b l", dict(c=2, b=2))
        xin = cut(4, 512, PAIR)
        cin = cut(2, 512, PAIR)
        xn = cut(2, 512, PAIR)
        x1 = cut(2, 512, PAIR)
        xn1 = cut(2, 512, PAIR)
        ct = cut(1, 512, FOUR)[0]
        FREQ = ("p (c r k) -> p c r k", dict(c=2, r=2))
        cf = cut(1, 512, FREQ)[0]
        fx = cut(1, 512, FREQ)[0]
        qs = cut(1, 512, ("p (r e) -> p r e", dict(r=2)))[0]
        prod = cut(1, 1024, ("p (k r e) -> p k r e", dict(k=2, r=2)))[0]
        vt = cut(2, 512, FOUR)
        mt = cut(1, 512, FOUR)[0]
        ot = cut(1, 512, FOUR)[0]
        SMALL = ("p (g k) -> p g k", dict(g=4))
        top = cut(2, 32, SMALL)
        lag = [v.bitcast(U32) for v in cut(2, 32, SMALL)]
        ex = cut(2, 16, SMALL)
        head_dim = cut(1, 16, SMALL)[0]
        head_dim_i = head_dim.bitcast(I32)
        shift = cut(1, 16, SMALL)[0]
        ssum = cut(1, 4, ("p (g k) -> p g k", dict(g=4)))[0]
        rsum = cut(1, 4, ("p (g k) -> p g k", dict(g=4)))[0]
        hot = cut(1, 256, ("p (g r k) -> p g r k", dict(g=4, r=HD)))[0]
        wsel = cut(1, 256, ("p (g r k) -> p g r k", dict(g=4, r=HD)))[0]
        w16 = cut(1, 64, ("p (g r) -> p g r", dict(g=4)))[0]
        wrep = cut(1, 512, ("p (g r h) -> p g r h", dict(g=4, r=HD)))[0]
        st1 = cut(1, 12, PAIR)[0]
        st2 = cut(1, 12, PAIR)[0]
        mv1 = cut(2, 4, PAIR)
        mv2 = cut(2, 4, PAIR)
        rs1 = cut(2, 2, ("p (b d) -> p b d", dict(b=2)))
        rs2 = cut(2, 2, ("p (b d) -> p b d", dict(b=2)))
        half = cut(1, 2, ("p (b d) -> p b d", dict(b=2)))[0]
        w_in_raw = arena[:, 0:DC * FF].rearrange("p (c f) -> p c f", c=DC)
        w_out_raw = arena[:, 2048:2048 + FC * D].rearrange("p (c n) -> p c n", c=FC)
        w_in_t = arena[:, 4096:4096 + FC * D].rearrange("p (c d) -> p c d", c=FC)
        w_tmp = arena[:, 6144:6144 + D].bitcast(I16)[:, 0:D]
        w_in_qt = arena[:, 6400:6400 + FC * D].rearrange("p (c d) -> p c d", c=FC)
        at = [0]
        xi = cut(1, 512, ("p (k) -> p k", {}))[0].bitcast(I16).rearrange("p (c n t) -> p c n t", c=2, n=2)
        hid = cut(4, 512, ("p (k) -> p k", {}))
        hq = [v.bitcast(I16) for v in cut(2, 256, ("p (k) -> p k", {}))]
        gbuf = [v.bitcast(F16).rearrange("p (s f t) -> p s f t", s=2, f=FC)
                for v in cut(2, FC * 512, ("p (k) -> p k", {}))]
        yq = cut(1, 2048, ("p (m b d) -> p m b d", dict(m=2, b=4)))[0]

        bank = [ctx.enter_context(nc.psum_tensor(f"bank{n}", [P, 512], F32)) for n in range(8)]
        four = lambda n: bank[n][:, :].rearrange("p (c b l) -> p c b l", c=2, b=2)
        freq = lambda n: bank[n][:, :].rearrange("p (c r b f) -> p c r b f", c=2, r=2, b=2)
        pair = lambda n: bank[n][:, :].rearrange("p (b d) -> p b d", b=2)
        ps_ct, ps_cf, ps_fx, ps_k, ps_q, ps_corr, ps_vt, ps_ot = (bank[n][:, :] for n in range(8))

        names = """const_in weights_in ffn_in w_in_turned w_in_copied w_in_small w_in_back w_in_ready
            half_ready rstd1 rstd2 ln1 ln1_stats ln2_stats front_ct front_cf front_fx
            ct_out cf_out fx_out v_done k_done q_done sc_top hd_done p_rstd1 p_rstd2 vt_out q_out prod_done inv_done top_done
            shift_done exp_done w16_done mt_done mt_out ot_done ot_out y_done x1_done xn1_done
            xnt_done xnt_out xmax_done x_chain w_chain ln_chain p_chain wo_chain sc_chain xmax_all
            x_scale wtop_all xi_done xhi_done xlo_done b_mm b_gelu b_max hmax_part hmax_all h_scale
            c_mm c_gelu c_hq c_hi c_lo c_y c_x1b c_out""".split()
        S = {n: sem("s_" + n) for n in names}
        s_x_in = [sem(f"s_x_in{n}") for n in range(4)]
        s_c_in = [sem(f"s_c_in{n}") for n in range(2)]
        s_x1_st = [sem(f"s_x1_st{n}") for n in range(2)]
        s_x1_ld = [sem(f"s_x1_ld{n}") for n in range(2)]
        s_out = [sem(f"s_out{n}") for n in range(2)]

        def wait(eng, s, n):
            if isinstance(n, int) and n <= 0:
                return
            eng.wait_ge(s, n)

        def upto(n):
            return min(n, PAIRS) if isinstance(n, int) else n

        s_passed = sem("s_passed")

        def wait_apart(eng, s, n):
            eng.wait_ge(s, n)
            if not isinstance(n, int):
                eng.sem_inc(s_passed, 1)

        def steps(eng, step):
            for t in range(UNROLL):
                step(t, t)
            with eng.Fori(1, PAIRS // UNROLL) as j:
                for k in range(UNROLL):
                    step(j * UNROLL + k, k)
            for t in range(PAIRS, PAIRS + LAST):
                step(t, t % UNROLL)

        def active(t, lagged):
            if isinstance(t, int):
                return 0 <= t - lagged < PAIRS
            return True

        block = ctx.enter_context(nc.Block())

        @block.sync
        def _(sp):
            sp.dma_start(cst[:, :], table).then_inc(S["const_in"], 16)
            sp.dma_start(w_in_raw, w_in.rearrange("(c p) f -> p c f", p=P)).then_inc(S["ffn_in"], 16)
            sp.dma_start(w_out_raw, w_out.rearrange("(c p) n -> p c n", p=P)).then_inc(S["ffn_in"], 16)
            sp.dma_start(b_in_sb[:, :], b_in.rearrange("(c p) -> p c", p=P), allow_slow_non_contiguous=True).then_inc(S["ffn_in"], 16)
            sp.dma_start(b_out_sb[:, :], b_out.rearrange("(a n) -> a n", a=1).broadcast_to([P, D])).then_inc(S["ffn_in"], 16)
            for n, w in enumerate((wq, wk, wv, wo)):
                sp.dma_start(w_attn[:, n, :, :], w.rearrange("(c p) n -> p c n", p=P)).then_inc(S["weights_in"], 16)
            sp.wait_ge(S["w_in_ready"], 2)

            def step(t, n):
                if active(t, 0):
                    wait(sp, S["x1_done"], t - 3)
                    sp.dma_start(xin[n], x_v[t, :, :, :] if isinstance(t, int) else x_v[bass.ds(t, 1), :, :, :].rearrange("n l b d -> (n l) b d")).then_inc(s_x_in[n], 16)
                    wait(sp, S["front_cf"], t - 1)
                    sp.dma_start(cin[n % 2], c_v[t, :, :, :] if isinstance(t, int) else c_v[bass.ds(t, 1), :, :, :].rearrange("n l b d -> (n l) b d")).then_inc(s_c_in[n % 2], 16)
                if active(t, 3):
                    p, m = t - 3, (n - 3) % 2
                    wait(sp, S["x1_done"], p + 1)
                    sp.dma_start(x1_v[p, :, :, :] if isinstance(t, int) else x1_v[bass.ds(p, 1), :, :, :].rearrange("n l b d -> (n l) b d"), x1[m]).then_inc(s_x1_st[m], 16)

            steps(sp, step)
            for m in range(2):
                sp.wait_ge(s_x1_st[m], 16 * (PAIRS // 2))
            sp.wait_ge(S["rstd2"], PAIRS)
            sp.wait_ge(S["xnt_out"], PAIRS)
            def load_x1(q, m):
                wait(sp, s_out[m], 16 * ((q - m) // 2) if isinstance(q, int) else (q - m) * 8)
                src = x1_q[q, :, :, :] if isinstance(q, int) else x1_q[bass.ds(q, 1), :, :, :].rearrange("n l b d -> (n l) b d")
                sp.dma_start(yq[:, m, :, :], src).then_inc(s_x1_ld[m], 16)

            def store(q, m):
                wait(sp, S["c_out"], q + 1)
                dst = out_q[q, :, :, :] if isinstance(q, int) else out_q[bass.ds(q, 1), :, :, :].rearrange("n l b d -> (n l) b d")
                sp.dma_start(dst, yq[:, m, :, :]).then_inc(s_out[m], 16)

            load_x1(0, 0)
            load_x1(1, 1)
            with sp.Fori(0, QUADS // 2 - 1) as i:
                for m in range(2):
                    store(i * 2 + m, m)
                    load_x1(i * 2 + (m + 2), m)
            store(QUADS - 2, 0)
            store(QUADS - 1, 1)
            for m in range(2):
                sp.wait_ge(s_out[m], 16 * (QUADS // 2))

        @block.tensor
        def _(pe):
            pe.wait_ge(S["const_in"], 16)
            pe.wait_ge(S["ffn_in"], 64)
            for f in range(FC):
                for c in range(DC):
                    last = nc.tensor.transpose(bank[f][:, c * P:(c + 1) * P], w_in_raw[:, c, f * P:(f + 1) * P], ident)
                last.then_inc(S["w_in_turned"], 1)
            for f in range(FC):
                pe.wait_ge(S["w_in_small"], f + 1)
                for c in range(DC):
                    last = nc.tensor.transpose(bank[f][:, c * P:(c + 1) * P], w_in_qt[:, f, c * P:(c + 1) * P], ident)
                last.then_inc(S["w_in_back"], 1)
            pe.wait_ge(S["weights_in"], 64)
            pe.wait_ge(S["w_in_ready"], 2)

            def dma_count(t, n, ring):
                return 16 * ((t - n) // ring + 1) if isinstance(t, int) else (t - n) * (16 // ring) + 16

            def front(p, n):
                m = n % 2
                wait(pe, s_c_in[m], dma_count(p, m, 2) if isinstance(p, int) else (p - m) * 8 + 16)
                wait(pe, S["x1_done"], p - 1)
                wait(pe, S["ct_out"], p)
                for c in range(DC):
                    for b in range(2):
                        last = nc.tensor.transpose(four(0)[:, c, b, :], cin[m][:, b, c * P:(c + 1) * P], ident)
                last.then_inc(S["front_ct"], 1)
                wait(pe, S["cf_out"], p)
                wait(pe, S["xnt_out"], p - 2)
                for c in range(DC):
                    for b in range(2):
                        last = nc.tensor.matmul(freq(1)[:, c, :, b, :], cin[m][:, b, c * P:(c + 1) * P], dft, start=True, stop=True)
                last.then_inc(S["front_cf"], 1)
                wait(pe, S["ln1"], p + 1)
                wait(pe, S["fx_out"], p)
                wait(pe, S["mt_out"], p - 1)
                for c in range(DC):
                    for b in range(2):
                        last = nc.tensor.matmul(freq(2)[:, c, :, b, :], xn[m][:, b, c * P:(c + 1) * P], dft, start=True, stop=True)
                last.then_inc(S["front_fx"], 1)

            def project(p, n):
                wait(pe, S["ct_out"], p + 1)
                wait(pe, S["vt_out"], p)
                for e in range(DC):
                    for c in range(DC):
                        last = nc.tensor.matmul(bank[6][:, e * D:(e + 1) * D], w_attn[:, 2, c, e * P:(e + 1) * P],
                                                ct[:, c, :, :].rearrange("p b l -> p (b l)"), start=c == 0, stop=c == DC - 1)
                last.then_inc(S["v_done"], 1)
                for which, src, b_, taken, w, done in ((1, cf, 3, "prod_done", 1, "k_done"), (0, fx, 4, "q_out", 0, "q_done")):
                    wait(pe, S["cf_out" if which else "fx_out"], p + 1)
                    wait(pe, S[taken], p)
                    for r in range(2):
                        for c in range(DC):
                            last = nc.tensor.matmul(bank[b_][:, r * D:(r + 1) * D], src[:, c, r, :],
                                                    w_attn[:, w, c, :], start=c == 0, stop=c == DC - 1)
                    last.then_inc(S[done], 1)

            def mixing(p, n):
                wait(pe, S["w16_done"], p + 1)
                wait(pe, S["fx_out"], upto(p + 2))
                for c in range(DC):
                    for b in range(2):
                        last = nc.tensor.transpose(four(2)[:, c, b, :], wrep[:, 2 * c + b, :, :].rearrange("p r h -> p (r h)"), ident)
                last.then_inc(S["mt_done"], 1)

            def turn_ln2(p, n):
                wait(pe, S["xn1_done"], p + 1)
                wait(pe, S["cf_out"], upto(p + 3))
                for c in range(DC):
                    for b in range(2):
                        last = nc.tensor.transpose(four(1)[:, c, b, :], xn1[n % 2][:, b, c * P:(c + 1) * P], ident)
                last.then_inc(S["xnt_done"], 1)

            def attend(p, n):
                wait(pe, S["mt_out"], p + 1)
                wait(pe, S["vt_out"], p + 1)
                wait(pe, S["ot_out"], p)
                for c in range(DC):
                    for b in range(2):
                        last = nc.tensor.matmul(four(7)[:, c, b, :], vt[n % 2][:, c, b, :], mt[:, c, b, :], start=True, stop=True)
                last.then_inc(S["ot_done"], 1)
                wait(pe, S["ot_out"], p + 1)
                wait(pe, S["ct_out"], upto(p + 2))
                for b in range(2):
                    for c in range(DC):
                        last = nc.tensor.matmul(pair(0)[:, b, :], ot[:, c, b, :], w_attn[:, 3, c, :], start=c == 0, stop=c == DC - 1)
                last.then_inc(S["y_done"], 1)

            def inverse(p, n):
                wait(pe, S["prod_done"], p + 1)
                wait(pe, S["top_done"], p)
                for e in range(DC):
                    for k in range(4):
                        last = nc.tensor.matmul(bank[5][:, e * D:(e + 1) * D], prod[:, k // 2, k % 2, e * P:(e + 1) * P],
                                                cst[:, C_INV + k * D:C_INV + (k + 1) * D], start=k == 0, stop=k == 3)
                last.then_inc(S["inv_done"], 1)

            def step(t, n):
                if active(t, 1):
                    front(t - 1, (n - 1) % 4)
                    project(t - 1, (n - 1) % 4)
                if active(t, 2):
                    mixing(t - 2, (n - 2) % 4)
                if active(t, 3):
                    turn_ln2(t - 3, (n - 3) % 4)
                if active(t, 2):
                    attend(t - 2, (n - 2) % 4)
                if active(t, 1):
                    inverse(t - 1, (n - 1) % 4)

            steps(pe, step)

            pe.wait_ge(S["top_done"], PAIRS)
            pe.wait_ge(S["x1_done"], PAIRS)
            pe.wait_ge(S["xnt_out"], PAIRS)

            def hidden(q, f, b):
                for s in range(2):
                    for c in range(DC):
                        rhs = xq[:, bass.ds(q, 1), s, c, :].rearrange("p q t -> p (q t)")
                        last = nc.tensor.matmul(bank[b][:, :], win16[:, c, f * P:(f + 1) * P], rhs,
                                                start=s == 0 and c == 0, stop=s == 1 and c == DC - 1)
                return last

            with pe.Fori(0, QUADS) as q:
                pe.wait_ge(S["xlo_done"], q + 1)
                for f in range(FC):
                    pe.wait_ge(S["b_gelu"], q * FC + (f + 1))
                    hidden(q, f, f).then_inc(S["b_mm"], 1)

            pe.wait_ge(S["b_gelu"], (QUADS + 1) * FC)

            def output(q, m, tchunk):
                wait(pe, S["c_lo"], (q + 1) * FC)
                wait(pe, S["c_out"], q)
                for f in range(FC):
                    for s in range(2):
                        last = nc.tensor.matmul(bank[4 + tchunk][:, 0:D], gbuf[m][:, s, f, tchunk * P:(tchunk + 1) * P],
                                                wout16[:, f, :], start=f == 0 and s == 0, stop=f == FC - 1 and s == 1)
                last.then_inc(S["c_y"], 1)

            def quad(q, m, has_hidden, has_output):
                for f in range(FC):
                    if has_hidden:
                        wait(pe, S["c_gelu"], q * FC + (f - 3))
                        hidden(q, f, f % 4).then_inc(S["c_mm"], 1)
                    if has_output and f % 2 == 1:
                        output(q - 1, 1 - m, f // 2)

            quad(0, 0, True, False)
            quad(1, 1, True, True)
            with pe.Fori(1, QUADS // 2) as i:
                quad(i * 2, 0, True, True)
                quad(i * 2 + 1, 1, True, True)
            quad(QUADS, 0, False, True)

        @block.scalar
        def _(act):
            def copy(dst, src, done):
                nc.scalar.activation(dst, src, ACT.Copy).then_inc(S[done], 1)

            act.wait_ge(S["w_in_ready"], 2)

            def step(t, n):
                if active(t, 1):
                    p = t - 1
                    act.wait_ge(S["front_ct"], p + 1)
                    wait(act, S["v_done"], p)
                    copy(ct.rearrange("p c b l -> p (c b l)"), bank[0][:, :], "ct_out")
                    act.wait_ge(S["front_cf"], p + 1)
                    wait(act, S["k_done"], p)
                    copy(cf.rearrange("p c r k -> p (c r k)"), bank[1][:, :], "cf_out")
                if active(t, 2):
                    p, m = t - 2, (n - 2) % 2
                    act.wait_ge(S["shift_done"], p + 1)
                    nc.scalar.activation(ex[m], shift, ACT.Exp).then_inc(S["exp_done"], 1)
                if active(t, 1):
                    p, m = t - 1, (n - 1) % 2
                    act.wait_ge(S["front_fx"], p + 1)
                    wait(act, S["q_done"], p)
                    copy(fx.rearrange("p c r k -> p (c r k)"), bank[2][:, :], "fx_out")
                    act.wait_ge(S["v_done"], p + 1)
                    wait(act, S["ot_done"], p - 1)
                    copy(vt[m].rearrange("p c b l -> p (c b l)"), bank[6][:, :], "vt_out")
                    act.wait_ge(S["q_done"], p + 1)
                    wait(act, S["prod_done"], p)
                    copy(qs.rearrange("p r e -> p (r e)"), bank[4][:, :], "q_out")
                if active(t, 3):
                    p = t - 3
                    act.wait_ge(S["xnt_done"], p + 1)
                    dst = xnt[:, p, :, :, :] if isinstance(p, int) else xnt[:, bass.ds(p, 1), :, :, :].rearrange("p n c b l -> p (n c) b l")
                    copy(dst, four(1), "xnt_out")
                if active(t, 2):
                    p = t - 2
                    act.wait_ge(S["ot_done"], p + 1)
                    wait(act, S["y_done"], p)
                    copy(ot.rearrange("p c b l -> p (c b l)"), bank[7][:, :], "ot_out")

            steps(act, step)

            act.wait_ge(S["x_scale"], 1)

            def gelu(dst, b, f, done):
                nc.scalar.activation(dst, bank[b][:, :], ACT.Gelu, bias=b_in_sb[:, f:f + 1],
                                     scale=z_scale[:, f:f + 1]).then_inc(S[done], 1)

            act.nop().then_inc(S["b_gelu"], FC)
            with act.Fori(0, QUADS) as q:
                for f in range(FC):
                    act.wait_ge(S["b_mm"], q * FC + (f + 1))
                    act.wait_ge(S["b_max"], q * FC + (f + 1))
                    gelu(hid[f % 4], f, f, "b_gelu")
            act.wait_ge(S["h_scale"], 1)
            def quad(q):
                for f in range(FC):
                    act.wait_ge(S["c_mm"], q * FC + (f + 1))
                    wait(act, S["c_hq"], q * FC + (f - 3))
                    gelu(hid[f % 4], f % 4, f, "c_gelu")
            quad(0)
            with act.Fori(1, QUADS) as q:
                quad(q)

        @block.gpsimd
        def _(pool):
            pool.wait_ge(S["wo_chain"], 3)
            nc.gpsimd.partition_all_reduce(wo_top, wo_part, P, RMAX).then_inc(S["wtop_all"], 1)
            pool.wait_ge(S["w_in_ready"], 2)
            nc.gpsimd.memset(half, -0.5).then_inc(S["half_ready"], 1)
            pool.wait_ge(S["half_ready"], 1)

            def rstd(p, m, mv, rs, stats, done):
                wait_apart(pool, S[stats], p + 1)
                nc.gpsimd.tensor_scalar(rs[m], mv[m][:, :, 1:2], EPS, None, ALU.add).then_inc(S["p_" + done], 1)
                pool.wait_ge(S["p_" + done], p + 1)
                nc.gpsimd.tensor_tensor(rs[m], rs[m], half, ALU.pow).then_inc(S[done], 1)

            def step(t, n):
                if active(t, 0):
                    rstd(t, n % 2, mv1, rs1, "ln1_stats", "rstd1")
                if active(t, 2):
                    rstd(t - 2, n % 2, mv2, rs2, "ln2_stats", "rstd2")

            steps(pool, step)
            pool.wait_ge(S["sc_chain"], 1)
            nc.gpsimd.partition_all_reduce(x_amax, xm_part, P, RMAX).then_inc(S["xmax_all"], 1)
            pool.wait_ge(S["hmax_part"], 1)
            nc.gpsimd.partition_all_reduce(h_amax, hm_part, P, RMAX).then_inc(S["hmax_all"], 1)
            def bias(q, m):
                wait(pool, s_x1_ld[m], 16 * ((q - m) // 2 + 1) if isinstance(q, int) else (q - m) * 8 + 16)
                nc.gpsimd.tensor_tensor(yq[:, m, :, :], yq[:, m, :, :], b_out_sb[:, :].unsqueeze(1).broadcast_to([P, 4, D]),
                                        ALU.add).then_inc(S["c_x1b"], 1)
            with pool.Fori(0, QUADS // 2) as i:
                bias(i * 2, 0)
                bias(i * 2 + 1, 1)

        @block.vector
        def _(dve):
            V = nc.vector
            dve.wait_ge(S["ffn_in"], 64)
            chain = [0]

            def link(ins):
                chain[0] += 1
                ins.then_inc(S["w_chain"], 1)
                dve.wait_ge(S["w_chain"], chain[0])

            V.tensor_reduce(wout_max[:, :], w_out_raw, AX_X, ALU.max, apply_absolute_value=True).then_inc(S["wo_chain"], 1)
            dve.wait_ge(S["wo_chain"], 1)
            V.tensor_scalar(wout_max[:, :], wout_max[:, :], TINY, None, ALU.max).then_inc(S["wo_chain"], 1)
            dve.wait_ge(S["wo_chain"], 2)
            V.tensor_reduce(wo_part, wout_max[:, :], AX_X, ALU.max).then_inc(S["wo_chain"], 1)
            link(V.reciprocal(wout_up[:, :], wout_max[:, :]))
            link(V.tensor_scalar(wout_up[:, :], wout_up[:, :], INT8, None, ALU.mult))
            for f in range(FC):
                link(V.tensor_scalar(w_tmp, w_out_raw[:, f, :], wout_up[:, f:f + 1], None, ALU.mult))
                link(V.tensor_copy(wout16[:, f, :], w_tmp))
            dve.wait_ge(S["wtop_all"], 1)
            link(V.reciprocal(wo_topr, wo_top))
            link(V.tensor_scalar(wout_rel[:, :], wout_max[:, :], wo_topr, None, ALU.mult))
            for f in range(FC):
                dve.wait_ge(S["w_in_turned"], f + 1)
                link(V.tensor_copy(w_in_t[:, f, :], bank[f][:, 0:D]))
                link(V.tensor_reduce(win_max[:, f:f + 1], w_in_t[:, f, :], AX_X, ALU.max, apply_absolute_value=True))
                link(V.tensor_scalar(win_max[:, f:f + 1], win_max[:, f:f + 1], TINY, None, ALU.max))
                link(V.reciprocal(win_up[:, f:f + 1], win_max[:, f:f + 1]))
                link(V.tensor_scalar(win_up[:, f:f + 1], win_up[:, f:f + 1], INT8, None, ALU.mult))
                link(V.tensor_scalar(w_tmp, w_in_t[:, f, :], win_up[:, f:f + 1], None, ALU.mult))
                V.tensor_copy(w_in_qt[:, f, :], w_tmp).then_inc(S["w_in_small"], 1)
                dve.wait_ge(S["w_in_small"], f + 1)
            for f in range(FC):
                dve.wait_ge(S["w_in_back"], f + 1)
                last = V.tensor_copy(win16[:, :, f * P:(f + 1) * P], bank[f][:, 0:D].rearrange("p (c e) -> p c e", c=DC))
            last.then_inc(S["w_in_ready"], 2)
            dve.wait_ge(S["w_in_ready"], 2)

            def norm1(t, n):
                m = n % 2
                wait(dve, s_x_in[n], 16 * (t // 4 + 1) if isinstance(t, int) else (t - n) * 4 + 16)
                for b in range(2):
                    last = V.bn_stats(st1[:, b, :], xin[n][:, b, :])
                last.then_inc(S["ln_chain"], 1)
                wait_apart(dve, S["ln_chain"], t + 1)
                for b in range(2):
                    last = V.bn_aggr(mv1[m][:, b, :], st1[:, b, :])
                last.then_inc(S["ln1_stats"], 1)

            def apply1(t, n):
                m = n % 2
                dve.wait_ge(S["rstd1"], t + 1)
                wait(dve, S["front_fx"], t - 1)
                for b in range(2):
                    last = V.tensor_scalar(xn[m][:, b, :], xin[n][:, b, :], mv1[m][:, b, 0:1], rs1[m][:, b, 0:1], ALU.subtract, ALU.mult)
                last.then_inc(S["ln1"], 1)

            def select(p, n):
                m = n % 2
                dve.wait_ge(S["exp_done"], p + 1)
                V.tensor_reduce(ssum[:, :, 0:1], ex[m], AX_X, ALU.add).then_inc(S["w_chain"], 1)
                V.tensor_tensor(hot, cst[:, C_IOTA:C_IOTA + HD].unsqueeze(1).unsqueeze(3).broadcast_to([P, 4, HD, KTOP]),
                                head_dim_i.unsqueeze(2).broadcast_to([P, 4, HD, KTOP]), ALU.is_equal).then_inc(S["w_chain"], 1)
                dve.wait_ge(S["w_chain"], p * 4 + (base + 2))
                V.reciprocal(rsum[:, :, 0:1], ssum[:, :, 0:1])
                V.tensor_tensor(wsel, hot, ex[m].unsqueeze(2).broadcast_to([P, 4, HD, KTOP]), ALU.mult).then_inc(S["w_chain"], 1)
                dve.wait_ge(S["w_chain"], p * 4 + (base + 3))
                V.tensor_reduce(w16, wsel, AX_X, ALU.add).then_inc(S["w_chain"], 1)
                dve.wait_ge(S["w_chain"], p * 4 + (base + 4))
                V.tensor_tensor(wrep, w16.unsqueeze(3).broadcast_to([P, 4, HD, NH]),
                                rsum.unsqueeze(3).broadcast_to([P, 4, HD, NH]), ALU.mult).then_inc(S["w16_done"], 1)

            def mix_out(p):
                dve.wait_ge(S["mt_done"], p + 1)
                wait(dve, S["ot_done"], p)
                V.tensor_tensor(mt.rearrange("p c b l -> p (c b) l"), four(2).rearrange("p c b l -> p (c b) l"),
                                mask.unsqueeze(1).broadcast_to([P, 4, P]), ALU.mult).then_inc(S["mt_out"], 1)

            def products(p):
                dve.wait_ge(S["q_out"], p + 1)
                dve.wait_ge(S["k_done"], p + 1)
                wait(dve, S["inv_done"], p)
                ps = bank[3][:, :].rearrange("p (r e) -> p r e", r=2)
                V.tensor_tensor(prod[:, 0, :, :], qs, ps, ALU.mult)
                for r in range(2):
                    last = V.tensor_tensor(prod[:, 1, r, :], qs[:, 1 - r, :], ps[:, r, :], ALU.mult)
                last.then_inc(S["prod_done"], 1)

            def residual(p, n):
                m = n % 2
                dve.wait_ge(S["y_done"], p + 1)
                if isinstance(p, int):
                    wait(dve, s_x1_st[m], 16 * ((p - m) // 2))
                else:
                    dve.wait_ge(s_x1_st[m], (p - m) * 8)
                V.tensor_tensor(x1[m], xin[n], pair(0), ALU.add).then_inc(S["x1_done"], 1)
                dve.wait_ge(S["x1_done"], p + 1)
                for b in range(2):
                    last = V.bn_stats(st2[:, b, :], x1[m][:, b, :])
                last.then_inc(S["x_chain"], 1)
                wait_apart(dve, S["x_chain"], p + 1)
                for b in range(2):
                    last = V.bn_aggr(mv2[m][:, b, :], st2[:, b, :])
                last.then_inc(S["ln2_stats"], 1)

            def apply2(p, n):
                m = n % 2
                dve.wait_ge(S["rstd2"], p + 1)
                if isinstance(p, int):
                    wait(dve, S["xnt_done"], p - 1)
                else:
                    dve.wait_ge(S["front_ct"], p + 2)
                for b in range(2):
                    last = V.tensor_scalar(xn1[m][:, b, :], x1[m][:, b, :], mv2[m][:, b, 0:1], rs2[m][:, b, 0:1], ALU.subtract, ALU.mult)
                last.then_inc(S["xn1_done"], 1)
                wait_apart(dve, S["xn1_done"], p + 1)
                V.tensor_reduce(xmax[:, bass.ds(p, 1)], xn1[m], AX_XY, ALU.max, apply_absolute_value=True)

            def top_lags(p, n):
                m = n % 2
                wait_apart(dve, S["inv_done"], p + 1)
                for g in range(4):
                    last = V.max(top[m][:, g, :], four(5)[:, g // 2, g % 2, :])
                last.then_inc(S["sc_top"], 1)
                dve.wait_ge(S["sc_top"], p * 2 + 1)
                V.tensor_tensor(shift, top[m][:, :, 0:KTOP], top[m][:, :, 0:1].broadcast_to([P, 4, KTOP]), ALU.subtract).then_inc(S["shift_done"], 1)
                for g in range(4):
                    last = V.max_index(lag[m][:, g, :], top[m][:, g, :], four(5)[:, g // 2, g % 2, :])
                last.then_inc(S["top_done"], 1)
                dve.wait_ge(S["top_done"], p + 1)
                V.scalar_tensor_tensor(head_dim_i, lag[m][:, :, 0:KTOP], -1.0, low.unsqueeze(1).broadcast_to([P, 4, KTOP]),
                                       ALU.mult, ALU.add).then_inc(S["sc_top"], 1)
                dve.wait_ge(S["sc_top"], p * 2 + 2)
                V.tensor_scalar(head_dim_i, head_dim_i, HD - 1, None, ALU.bitwise_and).then_inc(S["hd_done"], 1)

            base = chain[0]

            def step(t, n):
                if active(t, 2):
                    dve.wait_ge(S["hd_done"], t - 1)
                    select(t - 2, (n - 2) % 4)
                if active(t, 0):
                    norm1(t, n)
                if active(t, 3):
                    apply2(t - 3, (n - 3) % 4)
                if active(t, 0):
                    apply1(t, n)
                if active(t, 2):
                    mix_out(t - 2)
                if active(t, 1):
                    products(t - 1)
                if active(t, 2):
                    residual(t - 2, (n - 2) % 4)
                if active(t, 1):
                    top_lags(t - 1, (n - 1) % 4)

            steps(dve, step)

            sc = [0]

            def then(ins):
                sc[0] += 1
                ins.then_inc(S["sc_chain"], 1)
                dve.wait_ge(S["sc_chain"], sc[0])

            V.engine_nop().then_inc(S["xmax_done"], 1)
            dve.wait_ge(S["xmax_done"], 1)
            then(V.tensor_reduce(xm_part, xmax[:, :], AX_X, ALU.max))
            dve.wait_ge(S["xmax_all"], 1)
            then(V.tensor_scalar(x_amax, x_amax, TINY, None, ALU.max))
            then(V.reciprocal(x_up, x_amax))
            then(V.tensor_scalar(x_up, x_up, INT16, None, ALU.mult))
            then(V.tensor_scalar(z_scale[:, :], win_max[:, :], x_amax, 1.0 / INT8, ALU.mult, ALU.mult))
            V.tensor_scalar(z_scale[:, :], z_scale[:, :], 1.0 / INT16, None, ALU.mult).then_inc(S["x_scale"], 1)

            def round_x(q):
                src = xnt[:, bass.ds(q * 2, 2), :, :, :].rearrange("p n c b l -> p c n (b l)")
                wait(dve, S["xlo_done"], q)
                V.tensor_scalar(xi, src, x_up, None, ALU.mult).then_inc(S["xi_done"], 1)
                dve.wait_ge(S["xi_done"], q + 1)
                V.tensor_copy(xq[:, bass.ds(q, 1), 0, :, :].rearrange("p q c t -> p (q c t)"),
                              xi.rearrange("p c n t -> p (c n t)")).then_inc(S["xhi_done"], 1)
                dve.wait_ge(S["xhi_done"], q + 1)
                V.tensor_tensor(xq[:, bass.ds(q, 1), 1, :, :].rearrange("p q c t -> p (q c t)"),
                                xi.rearrange("p c n t -> p (c n t)"),
                                xq[:, bass.ds(q, 1), 0, :, :].rearrange("p q c t -> p (q c t)"),
                                ALU.subtract).then_inc(S["xlo_done"], 1)

            dve.wait_ge(S["xnt_out"], PAIRS)
            round_x(0)
            V.engine_nop().then_inc(S["b_max"], 4)

            def largest(q):
                for f in range(FC):
                    dve.wait_ge(S["b_gelu"], q * FC + (f + 1 + FC))
                    V.tensor_reduce(hmax[:, bass.ds(q, 1), f], hid[f % 4], AX_X, ALU.max, apply_absolute_value=True).then_inc(S["b_max"], 1)

            with dve.Fori(0, QUADS - 1) as q:
                round_x(q + 1)
                largest(q)
            largest(QUADS - 1)
            dve.wait_ge(S["b_max"], 4 + QUADS * FC)
            V.tensor_reduce(hm_part, hmax[:, :, :], AX_XY, ALU.max).then_inc(S["hmax_part"], 1)
            dve.wait_ge(S["hmax_all"], 1)
            then(V.tensor_scalar(h_amax, h_amax, TINY, None, ALU.max))
            then(V.reciprocal(h_up, h_amax))
            then(V.tensor_scalar(y_scale, h_amax, wo_top, 1.0 / INT8, ALU.mult, ALU.mult))
            then(V.tensor_scalar(y_scale, y_scale, 1.0 / INT16, None, ALU.mult))
            V.tensor_scalar(h_up, h_up, INT16, None, ALU.mult).then_inc(S["h_scale"], 1)
            dve.wait_ge(S["h_scale"], 1)

            def round_h(q, m):
                for f in range(FC):
                    dve.wait_ge(S["c_gelu"], q * FC + (f + 1))
                    V.tensor_scalar(hq[f % 2], hid[f % 4], h_up, None, ALU.mult).then_inc(S["c_hq"], 1)
                    if f == 0:
                        wait(dve, S["c_y"], (q - 1) * 4)
                    dve.wait_ge(S["c_hq"], q * FC + (f + 1))
                    V.tensor_scalar(gbuf[m][:, 0, f, :], hq[f % 2], wout_rel[:, f:f + 1], None, ALU.mult).then_inc(S["c_hi"], 1)
                    dve.wait_ge(S["c_hi"], q * FC + (f + 1))
                    V.scalar_tensor_tensor(gbuf[m][:, 1, f, :], hq[f % 2], wout_rel[:, f:f + 1], gbuf[m][:, 0, f, :],
                                           ALU.mult, ALU.subtract).then_inc(S["c_lo"], 1)

            def finish(q, m):
                dve.wait_ge(S["c_x1b"], q + 1)
                for k in range(4):
                    dve.wait_ge(S["c_y"], q * 4 + (k + 1))
                    last = V.scalar_tensor_tensor(yq[:, m, k, :], bank[4 + k][:, 0:D], y_scale, yq[:, m, k, :], ALU.mult, ALU.add)
                last.then_inc(S["c_out"], 1)

            for m in range(2):
                dve.wait_ge(s_x1_st[m], 16 * (PAIRS // 2))
            round_h(0, 0)
            round_h(1, 1)
            finish(0, 0)
            with dve.Fori(1, QUADS // 2) as i:
                round_h(i * 2, 0)
                finish(i * 2 - 1, 1)
                round_h(i * 2 + 1, 1)
                finish(i * 2, 0)
            finish(QUADS - 1, 1)


_INS = ["x", "ctx_1024", "L0_xattn_wq", "L0_xattn_wk", "L0_xattn_wv", "L0_xattn_wo",
        "L0_ffn_W_in", "L0_ffn_b_in", "L0_ffn_W_out", "L0_ffn_b_out"]


def kernel(**inputs):
    import numpy as _np
    import concourse.bacc as _bacc
    from concourse import mybir as _mybir
    from concourse.bass_utils import run_bass_kernel_spmd as _run

    nc = _bacc.Bacc("TRN2", target_bir_lowering=False, num_devices=1)
    arrays, args = {}, []
    for name in _INS:
        a = _np.asarray(inputs[name])
        if name[-2:] in ("wq", "wk", "wv"):
            a = a.reshape(2 * P, NH, 2, HD).transpose(0, 2, 3, 1).reshape(a.shape)
        a = _np.ascontiguousarray(a)
        arrays[f"in_{name}"] = a
        args.append(nc.dram_tensor(f"in_{name}", a.shape, _mybir.dt.from_np(a.dtype), kind="ExternalInput").ap())
    table = constants()
    arrays["table"] = table
    args.append(nc.dram_tensor("table", table.shape, _mybir.dt.float32, kind="ExternalInput").ap())
    shape = inputs["x"].shape
    args.append(nc.dram_tensor("out_0", shape, _mybir.dt.float32, kind="ExternalOutput").ap())
    args.append(nc.dram_tensor("x1_scratch", shape, _mybir.dt.float32, kind="Internal").ap())
    xattn_ffn_kernel(nc, *args)
    return _run(nc, [arrays], core_ids=[0]).results[0]["out_0"]
```

```python
from contextlib import ExitStack

import concourse.bass as bass
from concourse import mybir

ALU = mybir.AluOpType
ACT = mybir.ActivationFunctionType
F32 = mybir.dt.float32
F16 = mybir.dt.float16
I16 = mybir.dt.int16
I32 = mybir.dt.int32
U32 = mybir.dt.uint32
AX_X = mybir.AxisListType.X
AX_XY = mybir.AxisListType.XY
RMAX = bass.bass_isa.ReduceOp.max

P = 128
HD = 16
NH = P // HD
NF = P // 2
KTOP = 4
UNROLL = 4
PEELED = 8
LAST = 4
INT16 = 32767.0
INT8 = 127.0
TINY = 1e-8
EPS = 1e-5
OUT_AFTER = (2, 4, 6, 7)

C_DFT = 0
C_INV = C_DFT + P
C_ID = C_INV + 2 * 2 * P
C_MASK = C_ID + P
C_IOTA = C_MASK + P
C_LOW = C_IOTA + HD
C_KEEP = C_LOW + 1
C_ALL = C_KEEP + 3


def constants():
    import numpy as np
    t = np.arange(P)
    f = np.arange(NF)
    table = np.zeros((P, C_ALL), np.float64)
    angle = 2 * np.pi * np.outer(t, f) / P
    table[:, C_DFT:C_DFT + NF] = np.cos(angle)
    table[:, C_DFT + NF:C_DFT + P] = -np.sin(angle)
    table[:, C_DFT + NF] = np.cos(np.pi * t)
    cos = 2 * np.cos(angle.T) / P
    sin = 2 * np.sin(angle.T) / P
    cos[0] = 1.0 / P
    sin[0] = -np.cos(np.pi * t) / P
    for n, m in enumerate((cos, -sin)):
        at = C_INV + n * 2 * P
        for b in range(2):
            table[b * NF:(b + 1) * NF, at + b * P:at + (b + 1) * P] = m
    table[:, C_ID:C_ID + P] = np.eye(P)
    table[:, C_MASK:C_MASK + P] = (t[:, None] % NH) == (t[None, :] % NH)
    table[:, C_IOTA:C_IOTA + HD] = np.arange(HD)
    table[:, C_LOW] = t // NH + P
    keep = (t % NF != 0).astype(np.float64)
    table[:, C_KEEP] = keep
    table[:, C_KEEP + 1] = -keep
    table[:, C_KEEP + 2] = 1 - keep
    return table.astype(np.float32)


def xattn_ffn_kernel(nc, x, ctx_in, ctx_turned, wq, wk, wv, wo, w_in, b_in, w_out, b_out, table, out, x1_dram):
    B, L, D = x.shape
    FF = w_in.shape[0]
    DC = D // P
    FC = FF // P
    PAIRS = B // 2
    QUADS = B // 4
    assert L == P and DC == 2 and (PAIRS - PEELED) % UNROLL == 0 and QUADS % 2 == 0

    x_v = x.rearrange("(n b) l d -> n l b d", b=2)
    c_v = ctx_in.rearrange("(n b) l d -> n l b d", b=2)
    x1_v = x1_dram.rearrange("(n b) l d -> n l b d", b=2)
    x1_q = x1_dram.rearrange("(n b) l d -> n l b d", b=4)
    out_q = out.rearrange("(n b) l d -> n l b d", b=4)

    with ExitStack() as ctx:
        def sb(name, shape, dt):
            return ctx.enter_context(nc.sbuf_tensor(name, shape, dt))

        def sem(name):
            return ctx.enter_context(nc.semaphore(name))

        cst = sb("cst", [P, C_ALL], F32)
        dft = cst[:, C_DFT:C_DFT + P]
        ident = cst[:, C_ID:C_ID + P]
        mask = cst[:, C_MASK:C_MASK + P]
        low = cst[:, C_LOW:C_LOW + 1]
        keep = cst[:, C_KEEP:C_KEEP + 1]
        minus_keep = cst[:, C_KEEP + 1:C_KEEP + 2]
        drop = cst[:, C_KEEP + 2:C_KEEP + 3]
        w_attn = sb("w_attn", [P, 4, DC, D], F32)
        win16 = sb("win16", [P, DC, FF], F16)
        wout16 = sb("wout16", [P, FC, D], F16)
        xnt = sb("xnt", [P, PAIRS, DC, 2, P], F32)
        xq = xnt[:, :, :, :, :].bitcast(F16).rearrange("p n c b l -> p (n c b l)").rearrange(
            "p (q s c t) -> p q s c t", q=QUADS, s=2, c=DC)
        b_in_sb = sb("b_in_sb", [P, FC], F32)
        b_out_sb = sb("b_out_sb", [P, D], F32)
        xmax = sb("xmax", [P, PAIRS], F32)
        hmax = sb("hmax", [P, QUADS, FC], F32)
        win_max = sb("win_max", [P, FC], F32)
        win_up = sb("win_up", [P, FC], F32)
        wout_max = sb("wout_max", [P, FC], F32)
        wout_up = sb("wout_up", [P, FC], F32)
        wout_rel = sb("wout_rel", [P, FC], F32)
        z_scale = sb("z_scale", [P, FC], F32)
        one = sb("one", [P, 12], F32)
        x_amax, x_up, h_amax, h_up, y_scale, wo_top, wo_topr, wo_part, xm_part, hm_part = [
            one[:, n:n + 1] for n in range(10)]

        ARENA = 14336
        arena = sb("arena", [P, ARENA], F32)
        at = [0]

        def cut(n, words, shape):
            a = at[0]
            at[0] += n * words
            assert at[0] <= ARENA
            return [arena[:, a + k * words:a + (k + 1) * words].rearrange(shape[0], **shape[1]) for k in range(n)]

        PAIR = ("p (b d) -> p b d", dict(b=2))
        FOUR = ("p (c b l) -> p c b l", dict(c=2, b=2))
        xin = cut(4, 512, PAIR)
        cin = cut(2, 512, PAIR)
        cturn = cut(2, 512, ("p (c k) -> p c k", dict(c=2)))
        xn = cut(2, 512, PAIR)
        x1 = cut(2, 512, PAIR)
        xn1 = cut(2, 512, PAIR)
        FREQ = ("p (c r k) -> p c r k", dict(c=2, r=2))
        cf = cut(1, 512, FREQ)[0]
        fx = cut(1, 512, FREQ)[0]
        qs = cut(1, 768, ("p (r e) -> p r e", dict(r=3)))[0]
        prod = cut(1, 1024, ("p (k r e) -> p k r e", dict(k=2, r=2)))[0]
        csum = cut(1, 512, ("p (k e) -> p k e", dict(k=2)))[0]
        vt = cut(2, 512, FOUR)
        mt = cut(1, 512, FOUR)[0]
        ot = cut(1, 512, FOUR)[0]
        SMALL = ("p (g k) -> p g k", dict(g=4))
        top = cut(2, 32, SMALL)
        lag = [v.bitcast(U32) for v in cut(2, 32, SMALL)]
        ex = cut(2, 16, SMALL)
        head_dim = cut(1, 16, SMALL)[0]
        head_dim_i = head_dim.bitcast(I32)
        shift = cut(1, 16, SMALL)[0]
        ssum = cut(1, 4, ("p (g k) -> p g k", dict(g=4)))[0]
        rsum = cut(1, 4, ("p (g k) -> p g k", dict(g=4)))[0]
        hot = cut(1, 256, ("p (g r k) -> p g r k", dict(g=4, r=HD)))[0]
        wsel = cut(1, 256, ("p (g r k) -> p g r k", dict(g=4, r=HD)))[0]
        w16 = cut(1, 64, ("p (g r) -> p g r", dict(g=4)))[0]
        wrep = cut(1, 512, ("p (g r h) -> p g r h", dict(g=4, r=HD)))[0]
        st1 = cut(1, 12, PAIR)[0]
        st2 = cut(1, 12, PAIR)[0]
        mv1 = cut(2, 4, PAIR)
        mv2 = cut(2, 4, PAIR)
        rs1 = cut(2, 2, ("p (b d) -> p b d", dict(b=2)))
        rs2 = cut(2, 2, ("p (b d) -> p b d", dict(b=2)))
        nm1 = cut(2, 2, ("p (b d) -> p b d", dict(b=2)))
        nm2 = cut(2, 2, ("p (b d) -> p b d", dict(b=2)))
        half = cut(1, 2, ("p (b d) -> p b d", dict(b=2)))[0]
        RAW = 8 * 512
        w_in_raw = arena[:, RAW:RAW + FC * D].rearrange("p (c d) -> p c d", c=FC)
        w_out_raw = arena[:, RAW + 2048:RAW + 4096].rearrange("p (c n) -> p c n", c=FC)
        w_in_i = arena[:, RAW + 4096:RAW + 5120].bitcast(I16).rearrange("p (c d) -> p c d", c=FC)
        w_out_i = arena[:, RAW + 5120:RAW + 6144].bitcast(I16).rearrange("p (c d) -> p c d", c=FC)
        w_in_qt = arena[:, RAW + 6144:RAW + 8192].rearrange("p (c d) -> p c d", c=FC)
        at = [0]
        xi = cut(1, 512, ("p (k) -> p k", {}))[0].bitcast(I16).rearrange("p (c n t) -> p c n t", c=2, n=2)
        hid = cut(4, 512, ("p (k) -> p k", {}))
        hq = [v.bitcast(I16) for v in cut(2, 256, ("p (k) -> p k", {}))]
        gbuf = [v.bitcast(F16).rearrange("p (s f t) -> p s f t", s=2, f=FC)
                for v in cut(2, FC * 512, ("p (k) -> p k", {}))]
        yq = cut(1, 2048, ("p (m b d) -> p m b d", dict(m=2, b=4)))[0]

        bank = [ctx.enter_context(nc.psum_tensor(f"bank{n}", [P, 512], F32)) for n in range(8)]
        four = lambda n: bank[n][:, :].rearrange("p (c b l) -> p c b l", c=2, b=2)
        freq = lambda n: bank[n][:, :].rearrange("p (c r b f) -> p c r b f", c=2, r=2, b=2)
        pair = lambda n: bank[n][:, :].rearrange("p (b d) -> p b d", b=2)

        names = """const_in weights_in w_in_loaded ffn_in w_in_rounded w_in_back w_in_ready
            half_ready p1 p2 rstd1 rstd2 ln1 ln1_stats ln2_stats front_cf front_fx
            cf_out fx_out v_done k_done q_done vt_out q_out q_patched terms_done sums_done inv_done
            sc_top hd_done top_done shift_done exp_done w16_done wrep_done mt_done mt_out ot_done
            ot_out y_done x1_done xn1_done xnt_done xnt_out xmax_part x_chain w_chain ln_chain
            wo_chain sc_chain xmax_all xmax_done x_scale wtop_all xi_done xhi_done xlo_done b_mm
            b_gelu b_max hmax_part hmax_all h_scale c_mm c_gelu c_hq c_hi c_lo c_y c_x1b
            c_out""".split()
        S = {n: sem("s_" + n) for n in names}
        s_x_in = [sem(f"s_x_in{n}") for n in range(4)]
        s_t_in = [sem(f"s_t_in{n}") for n in range(2)]
        s_c_in = [sem(f"s_c_in{n}") for n in range(2)]
        s_x1_st = [sem(f"s_x1_st{n}") for n in range(2)]
        s_x1_ld = [sem(f"s_x1_ld{n}") for n in range(2)]
        s_out = [sem(f"s_out{n}") for n in range(2)]

        def wait(eng, s, n):
            if isinstance(n, int) and n <= 0:
                return
            eng.wait_ge(s, n)

        def upto(n):
            return min(n, PAIRS) if isinstance(n, int) else n

        s_passed = sem("s_passed")

        def wait_apart(eng, s, n):
            eng.wait_ge(s, n)
            if not isinstance(n, int):
                eng.sem_inc(s_passed, 1)

        def steps(eng, step):
            for t in range(PEELED):
                step(t, t % UNROLL)
            with eng.Fori(PEELED // UNROLL, PAIRS // UNROLL) as j:
                for k in range(UNROLL):
                    step(j * UNROLL + k, k)
            for t in range(PAIRS, PAIRS + LAST):
                step(t, t % UNROLL)

        def active(t, lagged):
            if isinstance(t, int):
                return 0 <= t - lagged < PAIRS
            return True

        block = ctx.enter_context(nc.Block())

        @block.sync
        def _(sp):
            sp.dma_start(w_in_raw, w_in.rearrange("(c p) d -> p c d", p=P)).then_inc(S["w_in_loaded"], 16)
            sp.dma_start(cst[:, :], table).then_inc(S["const_in"], 16)
            sp.dma_start(w_out_raw, w_out.rearrange("(c p) n -> p c n", p=P)).then_inc(S["ffn_in"], 16)

            def rows(v, p):
                if isinstance(p, int):
                    return v[p]
                names = "abcde"[:len(v.shape) - 1]
                return v[(bass.ds(p, 1),) + (slice(None),) * (len(v.shape) - 1)].rearrange(
                    f"n {' '.join(names)} -> (n {names[0]}) {' '.join(names[1:])}")

            def load(t, n):
                wait(sp, S["x1_done"], t - 3)
                sp.dma_start(xin[n], rows(x_v, t)).then_inc(s_x_in[n], 16)
                wait(sp, S["front_cf"], t - 1)
                sp.dma_start(cin[n % 2], rows(c_v, t)).then_inc(s_c_in[n % 2], 16)
                wait(sp, S["v_done"], t - 1)
                sp.dma_start(cturn[n % 2], rows(ctx_turned, t)).then_inc(s_t_in[n % 2], 16)

            load(0, 0)
            for n, w in enumerate((wq, wk, wv, wo)):
                sp.dma_start(w_attn[:, n, :, :], w.rearrange("(c p) n -> p c n", p=P)).then_inc(S["weights_in"], 16)
            load(1, 1)
            sp.dma_start(b_in_sb[:, :], b_in.rearrange("(c p) -> p c", p=P), allow_slow_non_contiguous=True).then_inc(S["ffn_in"], 16)
            sp.dma_start(b_out_sb[:, :], b_out.rearrange("(a n) -> a n", a=1).broadcast_to([P, D])).then_inc(S["ffn_in"], 16)

            def step(t, n):
                if active(t, 0) and not (isinstance(t, int) and t < 2):
                    load(t, n)
                if active(t, 4):
                    p, m = t - 4, n % 2
                    wait(sp, S["x1_done"], p + 1)
                    sp.dma_start(rows(x1_v, p), x1[m]).then_inc(s_x1_st[m], 16)

            steps(sp, step)
            for m in range(2):
                sp.wait_ge(s_x1_st[m], 16 * (PAIRS // 2))
            sp.wait_ge(S["rstd2"], PAIRS)
            sp.wait_ge(S["xnt_out"], PAIRS)
            def load_x1(q, m):
                wait(sp, s_out[m], 16 * ((q - m) // 2) if isinstance(q, int) else (q - m) * 8)
                sp.dma_start(yq[:, m, :, :], rows(x1_q, q)).then_inc(s_x1_ld[m], 16)

            def store(q, m):
                wait(sp, S["c_out"], q + 1)
                sp.dma_start(rows(out_q, q), yq[:, m, :, :]).then_inc(s_out[m], 16)

            load_x1(0, 0)
            load_x1(1, 1)
            with sp.Fori(0, QUADS // 2 - 1) as i:
                for m in range(2):
                    store(i * 2 + m, m)
                    load_x1(i * 2 + (m + 2), m)
            store(QUADS - 2, 0)
            store(QUADS - 1, 1)
            for m in range(2):
                sp.wait_ge(s_out[m], 16 * (QUADS // 2))

        @block.tensor
        def _(pe):
            pe.wait_ge(S["const_in"], 16)
            pe.wait_ge(S["w_in_rounded"], 1)
            for f in range(FC):
                for c in range(DC):
                    last = nc.tensor.transpose(bank[f][:, c * P:(c + 1) * P], w_in_qt[:, f, c * P:(c + 1) * P], ident)
                last.then_inc(S["w_in_back"], 1)
            pe.wait_ge(S["weights_in"], 64)
            pe.wait_ge(S["w_in_ready"], 2)

            def landed(t, n):
                return 16 * (t // 2 + 1) if isinstance(t, int) else (t - n % 2) * 8 + 16

            def dft_context(p, n):
                m = n % 2
                wait(pe, s_c_in[m], landed(p, n))
                wait(pe, S["cf_out"], p)
                for c in range(DC):
                    for b in range(2):
                        last = nc.tensor.matmul(freq(1)[:, c, :, b, :], cin[m][:, b, c * P:(c + 1) * P], dft, start=True, stop=True)
                last.then_inc(S["front_cf"], 1)

            def dft_norm(p, n):
                m = n % 2
                wait(pe, S["ln1"], p + 1)
                wait(pe, S["mt_out"], p - 1)
                for c in range(DC):
                    for b in range(2):
                        last = nc.tensor.matmul(freq(2)[:, c, :, b, :], xn[m][:, b, c * P:(c + 1) * P], dft, start=True, stop=True)
                last.then_inc(S["front_fx"], 1)

            def project(p, b_, src, ready, w, taken, done):
                wait(pe, S[ready], p + 1)
                wait(pe, S[taken], p)
                for r in range(2):
                    for c in range(DC):
                        last = nc.tensor.matmul(bank[b_][:, r * D:(r + 1) * D], src[:, c, r, :],
                                                w_attn[:, w, c, :], start=c == 0, stop=c == DC - 1)
                last.then_inc(S[done], 1)

            def project_v(p, n):
                m = n % 2
                wait(pe, s_t_in[m], landed(p, n))
                wait(pe, S["vt_out"], p)
                for e in range(DC):
                    for c in range(DC):
                        last = nc.tensor.matmul(bank[6][:, e * D:(e + 1) * D], w_attn[:, 2, c, e * P:(e + 1) * P],
                                                cturn[m][:, c, :], start=c == 0, stop=c == DC - 1)
                last.then_inc(S["v_done"], 1)

            def mixing(p):
                wait(pe, S["wrep_done"], p + 1)
                wait(pe, S["fx_out"], upto(p + 2))
                for c in range(DC):
                    for b in range(2):
                        last = nc.tensor.transpose(four(2)[:, c, b, :], wrep[:, 2 * c + b, :, :].rearrange("p r h -> p (r h)"), ident)
                last.then_inc(S["mt_done"], 1)

            def turn_ln2(p, n):
                wait(pe, S["xn1_done"], p + 1)
                wait(pe, S["ot_out"], upto(p + 2))
                for c in range(DC):
                    for b in range(2):
                        last = nc.tensor.transpose(four(7)[:, c, b, :], xn1[n % 2][:, b, c * P:(c + 1) * P], ident)
                last.then_inc(S["xnt_done"], 1)

            def attend(p, n):
                wait(pe, S["mt_out"], p + 1)
                wait(pe, S["vt_out"], p + 1)
                wait(pe, S["xnt_out"], p - 1)
                for c in range(DC):
                    for b in range(2):
                        last = nc.tensor.matmul(four(7)[:, c, b, :], vt[n % 2][:, c, b, :], mt[:, c, b, :], start=True, stop=True)
                last.then_inc(S["ot_done"], 1)

            def project_out(p):
                wait(pe, S["ot_out"], p + 1)
                wait(pe, S["x1_done"], p)
                for b in range(2):
                    for c in range(DC):
                        last = nc.tensor.matmul(pair(0)[:, b, :], ot[:, c, b, :], w_attn[:, 3, c, :], start=c == 0, stop=c == DC - 1)
                last.then_inc(S["y_done"], 1)

            def inverse(p):
                wait(pe, S["sums_done"], p + 1)
                wait(pe, S["top_done"], p)
                for e in range(DC):
                    for k in range(2):
                        last = nc.tensor.matmul(bank[5][:, e * D:(e + 1) * D], csum[:, k, e * P:(e + 1) * P],
                                                cst[:, C_INV + k * D:C_INV + (k + 1) * D], start=k == 0, stop=k == 1)
                last.then_inc(S["inv_done"], 1)

            def step(t, n):
                if active(t, 1):
                    dft_context(t - 1, n - 1)
                if active(t, 3):
                    mixing(t - 3)
                if active(t, 2):
                    inverse(t - 2)
                if active(t, 1):
                    dft_norm(t - 1, n - 1)
                if active(t, 3):
                    attend(t - 3, n - 3)
                if active(t, 1):
                    project(t - 1, 4, fx, "fx_out", 0, "q_patched", "q_done")
                    project(t - 1, 3, cf, "cf_out", 1, "terms_done", "k_done")
                if active(t, 3):
                    project_out(t - 3)
                if active(t, 1):
                    project_v(t - 1, n - 1)
                if active(t, 4):
                    turn_ln2(t - 4, n)

            steps(pe, step)

            pe.wait_ge(S["top_done"], PAIRS)
            pe.wait_ge(S["x1_done"], PAIRS)
            pe.wait_ge(S["xnt_out"], PAIRS)

            def hidden(q, f, b):
                for s in range(2):
                    for c in range(DC):
                        rhs = xq[:, bass.ds(q, 1), s, c, :].rearrange("p q t -> p (q t)")
                        last = nc.tensor.matmul(bank[b][:, :], win16[:, c, f * P:(f + 1) * P], rhs,
                                                start=s == 0 and c == 0, stop=s == 1 and c == DC - 1)
                return last

            with pe.Fori(0, QUADS) as q:
                pe.wait_ge(S["xlo_done"], q + 1)
                for f in range(FC):
                    pe.wait_ge(S["b_gelu"], q * FC + (f + 1))
                    hidden(q, f, f).then_inc(S["b_mm"], 1)

            pe.wait_ge(S["b_gelu"], (QUADS + 1) * FC)

            def output(q, m, tchunk):
                wait(pe, S["c_out"], q)
                for f in range(FC):
                    wait(pe, S["c_lo"], q * FC + (f + 1))
                    for s in range(2):
                        last = nc.tensor.matmul(bank[4 + tchunk][:, 0:D], gbuf[m][:, s, f, tchunk * P:(tchunk + 1) * P],
                                                wout16[:, f, :], start=f == 0 and s == 0, stop=f == FC - 1 and s == 1)
                last.then_inc(S["c_y"], 1)

            def quad(q, m, has_hidden, has_output):
                for f in range(FC):
                    if has_hidden:
                        wait(pe, S["c_gelu"], q * FC + (f - 3))
                        hidden(q, f, f % 4).then_inc(S["c_mm"], 1)
                    if has_output and f in OUT_AFTER:
                        output(q - 1, 1 - m, OUT_AFTER.index(f))

            quad(0, 0, True, False)
            quad(1, 1, True, True)
            with pe.Fori(1, QUADS // 2) as i:
                quad(i * 2, 0, True, True)
                quad(i * 2 + 1, 1, True, True)
            quad(QUADS, 0, False, True)

        @block.scalar
        def _(act):
            def copy(dst, src, done):
                nc.scalar.activation(dst, src, ACT.Copy).then_inc(S[done], 1)

            for f in range(FC // 2):
                act.wait_ge(S["w_in_back"], f + 1)
                last = nc.scalar.activation(win16[:, :, f * P:(f + 1) * P], bank[f][:, 0:D].rearrange("p (c e) -> p c e", c=DC), ACT.Copy)
            last.then_inc(S["w_in_ready"], 1)
            act.wait_ge(S["w_in_ready"], 2)

            def normalize(dst, src, rs, nm, done):
                for b in range(2):
                    last = nc.scalar.activation(dst[:, b, :], src[:, b, :], ACT.Identity, bias=nm[:, b, :], scale=rs[:, b, :])
                last.then_inc(S[done], 1)

            def step(t, n):
                if active(t, 1):
                    p = t - 1
                    act.wait_ge(S["front_cf"], p + 1)
                    wait(act, S["k_done"], p)
                    copy(cf.rearrange("p c r k -> p (c r k)"), bank[1][:, :], "cf_out")
                if active(t, 4):
                    p, m = t - 4, n % 2
                    act.wait_ge(S["rstd2"], p + 1)
                    wait(act, S["xmax_part"], p - 1)
                    wait(act, S["xnt_done"], p - 1)
                    normalize(xn1[m], x1[m], rs2[m], nm2[m], "xn1_done")
                if active(t, 1):
                    p = t - 1
                    act.wait_ge(S["front_fx"], p + 1)
                    wait(act, S["q_done"], p)
                    copy(fx.rearrange("p c r k -> p (c r k)"), bank[2][:, :], "fx_out")
                if active(t, 3):
                    p = t - 3
                    act.wait_ge(S["ot_done"], p + 1)
                    wait(act, S["y_done"], p)
                    copy(ot.rearrange("p c b l -> p (c b l)"), bank[7][:, :], "ot_out")
                if active(t, 2):
                    p, m = t - 2, n % 2
                    act.wait_ge(S["shift_done"], p + 1)
                    nc.scalar.activation(ex[m], shift, ACT.Exp).then_inc(S["exp_done"], 1)
                if active(t, 1):
                    p = t - 1
                    act.wait_ge(S["q_done"], p + 1)
                    wait(act, S["terms_done"], p)
                    nc.scalar.activation(qs[:, 0, :], bank[4][:, 0:D], ACT.Copy)
                    nc.scalar.activation(qs[:, 1, :], bank[4][:, D:2 * D], ACT.Copy, scale=keep)
                    nc.scalar.activation(qs[:, 2, :], bank[4][:, 0:D], ACT.Copy, scale=minus_keep).then_inc(S["q_out"], 1)
                if active(t, 0):
                    act.wait_ge(S["rstd1"], t + 1)
                    wait(act, S["front_fx"], t - 1)
                    normalize(xn[n % 2], xin[n], rs1[n % 2], nm1[n % 2], "ln1")
                if active(t, 2):
                    p = t - 2
                    act.wait_ge(S["w16_done"], p + 1)
                    wait(act, S["mt_done"], p)
                    copy(wrep, w16.unsqueeze(3).broadcast_to([P, 4, HD, NH]), "wrep_done")
                if active(t, 1):
                    p, m = t - 1, (n - 1) % 2
                    act.wait_ge(S["v_done"], p + 1)
                    wait(act, S["ot_done"], p - 1)
                    copy(vt[m].rearrange("p c b l -> p (c b l)"), bank[6][:, :], "vt_out")
                if active(t, 4):
                    p = t - 4
                    act.wait_ge(S["xnt_done"], p + 1)
                    dst = xnt[:, p, :, :, :] if isinstance(p, int) else xnt[:, bass.ds(p, 1), :, :, :].rearrange("p n c b l -> p (n c) b l")
                    copy(dst, four(7), "xnt_out")

            steps(act, step)

            act.wait_ge(S["x_scale"], 1)

            def gelu(dst, b, f, done):
                nc.scalar.activation(dst, bank[b][:, :], ACT.Gelu, bias=b_in_sb[:, f:f + 1],
                                     scale=z_scale[:, f:f + 1]).then_inc(S[done], 1)

            act.nop().then_inc(S["b_gelu"], FC)
            def first(q):
                for f in range(FC):
                    act.wait_ge(S["b_mm"], q * FC + (f + 1))
                    act.wait_ge(S["b_max"], q * FC + (f + 1))
                    gelu(hid[f % 4], f, f, "b_gelu")
            first(0)
            with act.Fori(1, QUADS) as q:
                first(q)
            act.wait_ge(S["h_scale"], 1)
            def quad(q):
                for f in range(FC):
                    act.wait_ge(S["c_mm"], q * FC + (f + 1))
                    wait(act, S["c_hq"], q * FC + (f - 3))
                    gelu(hid[f % 4], f % 4, f, "c_gelu")
            quad(0)
            with act.Fori(1, QUADS) as q:
                quad(q)

        @block.gpsimd
        def _(pool):
            pool.wait_ge(S["wo_chain"], 1)
            nc.gpsimd.partition_all_reduce(wo_top, wo_part, P, RMAX).then_inc(S["wtop_all"], 1)
            pool.wait_ge(S["w_in_ready"], 2)
            nc.gpsimd.memset(half, -0.5).then_inc(S["half_ready"], 1)
            pool.wait_ge(S["half_ready"], 1)

            def rstd(p, m, mv, rs, nm, stats, chain, taken, done):
                pool.wait_ge(S[stats], p + 1)
                wait_apart(pool, S[stats], p + 1)
                if not isinstance(p, int) or p > 1:
                    wait_apart(pool, S[taken], p - 1)
                nc.gpsimd.tensor_scalar(nm[m], mv[m][:, :, 0:1], -1.0, None, ALU.mult)
                nc.gpsimd.tensor_scalar(rs[m], mv[m][:, :, 1:2], EPS, None, ALU.add).then_inc(S[chain], 1)
                pool.wait_ge(S[chain], p * 2 + 1)
                nc.gpsimd.tensor_tensor(rs[m], rs[m], half, ALU.pow).then_inc(S[chain], 1)
                pool.wait_ge(S[chain], p * 2 + 2)
                nc.gpsimd.tensor_tensor(nm[m], nm[m], rs[m], ALU.mult).then_inc(S[done], 1)

            def step(t, n):
                if active(t, 4):
                    rstd(t - 4, n % 2, mv2, rs2, nm2, "ln2_stats", "p2", "xn1_done", "rstd2")
                if active(t, 0):
                    rstd(t, n % 2, mv1, rs1, nm1, "ln1_stats", "p1", "ln1", "rstd1")
                if active(t, 1):
                    p = t - 1
                    pool.wait_ge(S["terms_done"], p + 1)
                    wait(pool, S["inv_done"], p)
                    nc.gpsimd.tensor_tensor(csum, prod[:, :, 0, :], prod[:, :, 1, :], ALU.add).then_inc(S["sums_done"], 1)

            steps(pool, step)
            pool.wait_ge(S["sc_chain"], 1)
            nc.gpsimd.partition_all_reduce(x_amax, xm_part, P, RMAX).then_inc(S["xmax_all"], 1)
            pool.wait_ge(S["hmax_part"], 1)
            nc.gpsimd.partition_all_reduce(h_amax, hm_part, P, RMAX).then_inc(S["hmax_all"], 1)
            def bias(q, m):
                wait(pool, s_x1_ld[m], 16 * ((q - m) // 2 + 1) if isinstance(q, int) else (q - m) * 8 + 16)
                nc.gpsimd.tensor_tensor(yq[:, m, :, :], yq[:, m, :, :], b_out_sb[:, :].unsqueeze(1).broadcast_to([P, 4, D]),
                                        ALU.add).then_inc(S["c_x1b"], 1)
            with pool.Fori(0, QUADS // 2) as i:
                bias(i * 2, 0)
                bias(i * 2 + 1, 1)

        @block.vector
        def _(dve):
            V = nc.vector
            chain = [0]

            def link(ins):
                chain[0] += 1
                ins.then_inc(S["w_chain"], 1)
                dve.wait_ge(S["w_chain"], chain[0])

            def round_rows(raw, top_, up, ints):
                link(V.tensor_reduce(top_[:, :], raw, AX_X, ALU.max, apply_absolute_value=True))
                link(V.tensor_scalar(top_[:, :], top_[:, :], TINY, None, ALU.max))
                link(V.reciprocal(up[:, :], top_[:, :]))
                link(V.tensor_scalar(up[:, :], up[:, :], INT8, None, ALU.mult))
                link(V.tensor_tensor(ints, raw, up[:, :].unsqueeze(2).broadcast_to([P, FC, D]), ALU.mult))

            dve.wait_ge(S["w_in_loaded"], 16)
            round_rows(w_in_raw, win_max, win_up, w_in_i)
            V.tensor_copy(w_in_qt, w_in_i).then_inc(S["w_in_rounded"], 1)
            dve.wait_ge(S["ffn_in"], 48)
            round_rows(w_out_raw, wout_max, wout_up, w_out_i)
            V.tensor_copy(wout16[:, :, :], w_out_i)
            V.tensor_reduce(wo_part, wout_max[:, :], AX_X, ALU.max).then_inc(S["wo_chain"], 1)
            for f in range(FC // 2, FC):
                dve.wait_ge(S["w_in_back"], f + 1)
                last = V.tensor_copy(win16[:, :, f * P:(f + 1) * P], bank[f][:, 0:D].rearrange("p (c e) -> p c e", c=DC))
            last.then_inc(S["w_in_ready"], 1)
            dve.wait_ge(S["wtop_all"], 1)
            link(V.reciprocal(wo_topr, wo_top))
            link(V.tensor_scalar(wout_rel[:, :], wout_max[:, :], wo_topr, None, ALU.mult))
            dve.wait_ge(S["w_in_ready"], 2)

            def norm1(t, n):
                m = n % 2
                wait(dve, s_x_in[n], 16 * (t // 4 + 1) if isinstance(t, int) else (t - n) * 4 + 16)
                wait(dve, S["ln1_stats"], t)
                for b in range(2):
                    last = V.bn_stats(st1[:, b, :], xin[n][:, b, :])
                last.then_inc(S["ln_chain"], 1)
                wait_apart(dve, S["ln_chain"], t + 1)
                if not isinstance(t, int) or t > 1:
                    wait_apart(dve, S["rstd1"], t - 1)
                for b in range(2):
                    last = V.bn_aggr(mv1[m][:, b, :], st1[:, b, :])
                last.then_inc(S["ln1_stats"], 1)

            def select(p, n):
                m = n % 2
                dve.wait_ge(S["hd_done"], p + 1)
                V.tensor_tensor(hot, cst[:, C_IOTA:C_IOTA + HD].unsqueeze(1).unsqueeze(3).broadcast_to([P, 4, HD, KTOP]),
                                head_dim_i.unsqueeze(2).broadcast_to([P, 4, HD, KTOP]), ALU.is_equal).then_inc(S["w_chain"], 1)
                dve.wait_ge(S["exp_done"], p + 1)
                V.tensor_reduce(ssum[:, :, 0:1], ex[m], AX_X, ALU.add).then_inc(S["w_chain"], 1)
                dve.wait_ge(S["w_chain"], p * 5 + (base + 1))
                V.tensor_tensor(wsel, hot, ex[m].unsqueeze(2).broadcast_to([P, 4, HD, KTOP]), ALU.mult).then_inc(S["w_chain"], 1)
                dve.wait_ge(S["w_chain"], p * 5 + (base + 2))
                V.reciprocal(rsum[:, :, 0:1], ssum[:, :, 0:1]).then_inc(S["w_chain"], 1)
                dve.wait_ge(S["w_chain"], p * 5 + (base + 3))
                wait(dve, S["wrep_done"], p)
                V.tensor_reduce(w16, wsel, AX_X, ALU.add).then_inc(S["w_chain"], 1)
                dve.wait_ge(S["w_chain"], p * 5 + (base + 5))
                V.tensor_tensor(w16, w16, rsum[:, :, 0:1].broadcast_to([P, 4, HD]), ALU.mult).then_inc(S["w16_done"], 1)

            def mix_out(p):
                dve.wait_ge(S["mt_done"], p + 1)
                wait(dve, S["ot_done"], p)
                V.tensor_tensor(mt.rearrange("p c b l -> p (c b) l"), four(2).rearrange("p c b l -> p (c b) l"),
                                mask.unsqueeze(1).broadcast_to([P, 4, P]), ALU.mult).then_inc(S["mt_out"], 1)

            def products(p):
                dve.wait_ge(S["q_out"], p + 1)
                V.scalar_tensor_tensor(qs[:, 2, :], bank[4][:, D:2 * D], drop, qs[:, 2, :], ALU.mult, ALU.add).then_inc(S["q_patched"], 1)
                dve.wait_ge(S["k_done"], p + 1)
                wait(dve, S["sums_done"], p)
                ps = bank[3][:, :].rearrange("p (r e) -> p r e", r=2)
                V.tensor_tensor(prod[:, 0, :, :], qs[:, 0:2, :], ps, ALU.mult)
                dve.wait_ge(S["q_patched"], p + 1)
                V.tensor_tensor(prod[:, 1, :, :], qs[:, 1:3, :], ps, ALU.mult).then_inc(S["terms_done"], 1)

            def residual(p, n):
                m = n % 2
                dve.wait_ge(S["y_done"], p + 1)
                if isinstance(p, int):
                    wait(dve, s_x1_st[m], 16 * ((p - m) // 2))
                else:
                    dve.wait_ge(s_x1_st[m], (p - m) * 8)
                wait(dve, S["xn1_done"], p - 1)
                V.tensor_tensor(x1[m], xin[n], pair(0), ALU.add).then_inc(S["x1_done"], 1)
                dve.wait_ge(S["x1_done"], p + 1)
                wait(dve, S["ln2_stats"], p)
                for b in range(2):
                    last = V.bn_stats(st2[:, b, :], x1[m][:, b, :])
                last.then_inc(S["x_chain"], 1)
                wait_apart(dve, S["x_chain"], p + 1)
                if not isinstance(p, int) or p > 1:
                    wait_apart(dve, S["rstd2"], p - 1)
                for b in range(2):
                    last = V.bn_aggr(mv2[m][:, b, :], st2[:, b, :])
                last.then_inc(S["ln2_stats"], 1)

            def magnitude(p, n):
                wait_apart(dve, S["xn1_done"], p + 1)
                V.tensor_reduce(xmax[:, bass.ds(p, 1)], xn1[n % 2], AX_XY, ALU.max, apply_absolute_value=True).then_inc(S["xmax_part"], 1)

            def top_lags(p, n):
                m = n % 2
                wait_apart(dve, S["inv_done"], p + 1)
                for g in range(4):
                    last = V.max(top[m][:, g, :], four(5)[:, g // 2, g % 2, :])
                last.then_inc(S["sc_top"], 1)
                dve.wait_ge(S["sc_top"], p * 2 + 1)
                V.tensor_tensor(shift, top[m][:, :, 0:KTOP], top[m][:, :, 0:1].broadcast_to([P, 4, KTOP]), ALU.subtract).then_inc(S["shift_done"], 1)
                for g in range(4):
                    last = V.max_index(lag[m][:, g, :], top[m][:, g, :], four(5)[:, g // 2, g % 2, :])
                last.then_inc(S["top_done"], 1)
                dve.wait_ge(S["top_done"], p + 1)
                V.scalar_tensor_tensor(head_dim_i, lag[m][:, :, 0:KTOP], -1.0, low.unsqueeze(1).broadcast_to([P, 4, KTOP]),
                                       ALU.mult, ALU.add).then_inc(S["sc_top"], 1)
                dve.wait_ge(S["sc_top"], p * 2 + 2)
                V.tensor_scalar(head_dim_i, head_dim_i, HD - 1, None, ALU.bitwise_and).then_inc(S["hd_done"], 1)

            base = chain[0]

            def step(t, n):
                if active(t, 3):
                    mix_out(t - 3)
                if active(t, 2):
                    top_lags(t - 2, n - 2)
                if active(t, 0):
                    norm1(t, n)
                if active(t, 2):
                    select(t - 2, n - 2)
                if active(t, 4):
                    magnitude(t - 4, n)
                if active(t, 1):
                    products(t - 1)
                if active(t, 3):
                    residual(t - 3, (n - 3) % 4)

            steps(dve, step)

            sc = [0]

            def then(ins):
                sc[0] += 1
                ins.then_inc(S["sc_chain"], 1)
                dve.wait_ge(S["sc_chain"], sc[0])

            dve.wait_ge(S["xmax_part"], PAIRS)
            then(V.tensor_reduce(xm_part, xmax[:, :], AX_X, ALU.max))
            dve.wait_ge(S["xmax_all"], 1)
            then(V.tensor_scalar(x_amax, x_amax, TINY, None, ALU.max))
            then(V.reciprocal(x_up, x_amax))
            then(V.tensor_scalar(x_up, x_up, INT16, None, ALU.mult))
            then(V.tensor_scalar(z_scale[:, :], win_max[:, :], x_amax, 1.0 / INT8, ALU.mult, ALU.mult))
            V.tensor_scalar(z_scale[:, :], z_scale[:, :], 1.0 / INT16, None, ALU.mult).then_inc(S["x_scale"], 1)

            def round_x(q):
                src = xnt[:, bass.ds(q * 2, 2), :, :, :].rearrange("p n c b l -> p c n (b l)")
                wait(dve, S["xlo_done"], q)
                V.tensor_scalar(xi, src, x_up, None, ALU.mult).then_inc(S["xi_done"], 1)
                dve.wait_ge(S["xi_done"], q + 1)
                V.tensor_copy(xq[:, bass.ds(q, 1), 0, :, :].rearrange("p q c t -> p (q c t)"),
                              xi.rearrange("p c n t -> p (c n t)")).then_inc(S["xhi_done"], 1)
                dve.wait_ge(S["xhi_done"], q + 1)
                V.tensor_tensor(xq[:, bass.ds(q, 1), 1, :, :].rearrange("p q c t -> p (q c t)"),
                                xi.rearrange("p c n t -> p (c n t)"),
                                xq[:, bass.ds(q, 1), 0, :, :].rearrange("p q c t -> p (q c t)"),
                                ALU.subtract).then_inc(S["xlo_done"], 1)

            dve.wait_ge(S["xnt_out"], PAIRS)
            round_x(0)
            V.engine_nop().then_inc(S["b_max"], 4)

            def largest(q):
                for f in range(FC):
                    dve.wait_ge(S["b_gelu"], q * FC + (f + 1 + FC))
                    V.tensor_reduce(hmax[:, bass.ds(q, 1), f], hid[f % 4], AX_X, ALU.max, apply_absolute_value=True).then_inc(S["b_max"], 1)

            with dve.Fori(0, QUADS - 1) as q:
                round_x(q + 1)
                largest(q)
            largest(QUADS - 1)
            dve.wait_ge(S["b_max"], 4 + QUADS * FC)
            V.tensor_reduce(hm_part, hmax[:, :, :], AX_XY, ALU.max).then_inc(S["hmax_part"], 1)
            dve.wait_ge(S["hmax_all"], 1)
            then(V.tensor_scalar(h_amax, h_amax, TINY, None, ALU.max))
            then(V.reciprocal(h_up, h_amax))
            then(V.tensor_scalar(y_scale, h_amax, wo_top, 1.0 / INT8, ALU.mult, ALU.mult))
            then(V.tensor_scalar(y_scale, y_scale, 1.0 / INT16, None, ALU.mult))
            V.tensor_scalar(h_up, h_up, INT16, None, ALU.mult).then_inc(S["h_scale"], 1)
            dve.wait_ge(S["h_scale"], 1)

            def round_h(q, m):
                for f in range(FC):
                    dve.wait_ge(S["c_gelu"], q * FC + (f + 1))
                    V.tensor_scalar(hq[f % 2], hid[f % 4], h_up, None, ALU.mult).then_inc(S["c_hq"], 1)
                    if f == 0:
                        wait(dve, S["c_y"], (q - 1) * 4)
                    dve.wait_ge(S["c_hq"], q * FC + (f + 1))
                    V.tensor_scalar(gbuf[m][:, 0, f, :], hq[f % 2], wout_rel[:, f:f + 1], None, ALU.mult).then_inc(S["c_hi"], 1)
                    dve.wait_ge(S["c_hi"], q * FC + (f + 1))
                    V.scalar_tensor_tensor(gbuf[m][:, 1, f, :], hq[f % 2], wout_rel[:, f:f + 1], gbuf[m][:, 0, f, :],
                                           ALU.mult, ALU.subtract).then_inc(S["c_lo"], 1)

            def finish(q, m):
                dve.wait_ge(S["c_x1b"], q + 1)
                for k in range(4):
                    dve.wait_ge(S["c_y"], q * 4 + (k + 1))
                    last = V.scalar_tensor_tensor(yq[:, m, k, :], bank[4 + k][:, 0:D], y_scale, yq[:, m, k, :], ALU.mult, ALU.add)
                last.then_inc(S["c_out"], 1)

            for m in range(2):
                dve.wait_ge(s_x1_st[m], 16 * (PAIRS // 2))
            round_h(0, 0)
            round_h(1, 1)
            finish(0, 0)
            with dve.Fori(1, QUADS // 2) as i:
                round_h(i * 2, 0)
                finish(i * 2 - 1, 1)
                round_h(i * 2 + 1, 1)
                finish(i * 2, 0)
            finish(QUADS - 1, 1)


_INS = ["x", "ctx_1024", "ctx_turned", "L0_xattn_wq", "L0_xattn_wk", "L0_xattn_wv", "L0_xattn_wo",
        "L0_ffn_W_in", "L0_ffn_b_in", "L0_ffn_W_out", "L0_ffn_b_out"]


def kernel(**inputs):
    import numpy as _np
    import concourse.bacc as _bacc
    from concourse import mybir as _mybir
    from concourse.bass_utils import run_bass_kernel_spmd as _run

    nc = _bacc.Bacc("TRN2", target_bir_lowering=False, num_devices=1)
    arrays, args = {}, []
    c = _np.asarray(inputs["ctx_1024"])
    turned = c.reshape(c.shape[0] // 2, 2, P, 2, P).transpose(0, 4, 3, 1, 2).reshape(-1, P, 2, 2 * P)
    inputs = dict(inputs, ctx_turned=turned)
    for name in _INS:
        a = _np.asarray(inputs[name])
        if name.endswith("W_in"):
            a = a.T
        if name[-2:] in ("wq", "wk", "wv"):
            a = a.reshape(2 * P, NH, 2, HD).transpose(0, 2, 3, 1).reshape(a.shape)
        a = _np.ascontiguousarray(a)
        arrays[f"in_{name}"] = a
        args.append(nc.dram_tensor(f"in_{name}", a.shape, _mybir.dt.from_np(a.dtype), kind="ExternalInput").ap())
    table = constants()
    arrays["table"] = table
    args.append(nc.dram_tensor("table", table.shape, _mybir.dt.float32, kind="ExternalInput").ap())
    shape = inputs["x"].shape
    args.append(nc.dram_tensor("out_0", shape, _mybir.dt.float32, kind="ExternalOutput").ap())
    args.append(nc.dram_tensor("x1_scratch", shape, _mybir.dt.float32, kind="Internal").ap())
    xattn_ffn_kernel(nc, *args)
    return _run(nc, [arrays], core_ids=[0]).results[0]["out_0"]
```

```python
from contextlib import ExitStack

import concourse.bass as bass
from concourse import mybir

ALU = mybir.AluOpType
ACT = mybir.ActivationFunctionType
F32 = mybir.dt.float32
F16 = mybir.dt.float16
I16 = mybir.dt.int16
I32 = mybir.dt.int32
U32 = mybir.dt.uint32
AX_X = mybir.AxisListType.X
AX_XY = mybir.AxisListType.XY
RMAX = bass.bass_isa.ReduceOp.max

P = 128
HD = 16
NH = P // HD
NF = P // 2
KTOP = 4
UNROLL = 8
PEELED = 8
LAST = 5
INT16 = 32767.0
INT8 = 127.0
TINY = 1e-8
EPS = 1e-5
SAVED = 4
FINISH_AT = 4
OUT_AFTER = (5, 6, 7, 7)

C_DFT = 0
C_ID = C_DFT + P
C_MASK = C_ID + P
C_IOTA = C_MASK + P
C_LOW = C_IOTA + HD
C_KEEP = C_LOW + 1
C_ALL = C_KEEP + 3


W_UP = 64.0
Q_DOWN = 2.0 ** -22
G_UP = P / 2.0
CORR_UP = W_UP * W_UP * Q_DOWN * G_UP


def constants():
    import numpy as np
    t = np.arange(P)
    f = np.arange(NF)
    table = np.zeros((P, C_ALL), np.float64)
    angle = 2 * np.pi * np.outer(t, f) / P
    table[:, C_DFT:C_DFT + NF] = np.cos(angle)
    table[:, C_DFT + NF:C_DFT + P] = -np.sin(angle)
    table[:, C_DFT + NF] = np.cos(np.pi * t)
    cos = 2 * np.cos(angle.T) / P
    sin = 2 * np.sin(angle.T) / P
    cos[0] = 1.0 / P
    sin[0] = -np.cos(np.pi * t) / P
    inverse = np.zeros((P, 2, 2 * P))
    for n, m in enumerate((cos, -sin)):
        for b in range(2):
            inverse[b * NF:(b + 1) * NF, n, b * P:(b + 1) * P] = m * G_UP
    inv16 = np.zeros((P, 2, 2, 2 * P), np.float16)
    inv16[:, 0] = inverse
    inv16[:, 1] = inverse - inv16[:, 0]
    table[:, C_ID:C_ID + P] = np.eye(P)
    table[:, C_MASK:C_MASK + P] = (t[:, None] % NH) == (t[None, :] % NH)
    table[:, C_IOTA:C_IOTA + HD] = np.arange(HD)
    table[:, C_LOW] = t // NH + P
    keep = (t % NF != 0).astype(np.float64)
    table[:, C_KEEP] = keep * Q_DOWN
    table[:, C_KEEP + 1] = -keep * Q_DOWN
    table[:, C_KEEP + 2] = (1 - keep) * Q_DOWN
    return table.astype(np.float32), inv16


def xattn_ffn_kernel(nc, x, ctx_in, ctx_turned, wq, wk, wv, wo, w_in, b_in, w_out, b_out, table, inv_table, out, x1_dram, h_dram):
    B, L, D = x.shape
    FF = w_in.shape[0]
    DC = D // P
    FC = FF // P
    PAIRS = B // 2
    QUADS = B // 4
    assert L == P and DC == 2 and (PAIRS - PEELED) % UNROLL == 0 and QUADS % 2 == 0

    x_v = x.rearrange("(n b) l d -> n l b d", b=2)
    c_v = ctx_in.rearrange("(n b) l d -> n l b d", b=2)
    x1_v = x1_dram.rearrange("(n b) l d -> n l b d", b=2)
    x1_q = x1_dram.rearrange("(n b) l d -> n l b d", b=4)
    out_q = out.rearrange("(n b) l d -> n l b d", b=4)

    with ExitStack() as ctx:
        def sb(name, shape, dt):
            return ctx.enter_context(nc.sbuf_tensor(name, shape, dt))

        def sem(name):
            return ctx.enter_context(nc.semaphore(name))

        cst = sb("cst", [P, C_ALL], F32)
        dft = cst[:, C_DFT:C_DFT + P]
        ident = cst[:, C_ID:C_ID + P]
        mask = cst[:, C_MASK:C_MASK + P]
        low = cst[:, C_LOW:C_LOW + 1]
        keep = cst[:, C_KEEP:C_KEEP + 1]
        minus_keep = cst[:, C_KEEP + 1:C_KEEP + 2]
        drop = cst[:, C_KEEP + 2:C_KEEP + 3]
        w16 = sb("w16", [P, 2, 4, DC, D], F16)
        inv16 = sb("inv16", [P, 2, 2, 2 * P], F16)
        win16 = sb("win16", [P, DC, FF], F16)
        wout16 = sb("wout16", [P, FC, D], F16)
        xnt = sb("xnt", [P, PAIRS, DC, 2, P], F32)
        xq = xnt[:, :, :, :, :].bitcast(F16).rearrange("p n c b l -> p (n c b l)").rearrange(
            "p (q s c t) -> p q s c t", q=QUADS, s=2, c=DC)
        b_in_sb = sb("b_in_sb", [P, FC], F32)
        b_out_sb = sb("b_out_sb", [P, D], F32)
        xmax = sb("xmax", [P, PAIRS], F32)
        hmax = sb("hmax", [P, QUADS, FC], F32)
        win_max = sb("win_max", [P, FC], F32)
        win_up = sb("win_up", [P, FC], F32)
        wout_max = sb("wout_max", [P, FC], F32)
        wout_up = sb("wout_up", [P, FC], F32)
        wout_rel = sb("wout_rel", [P, FC], F32)
        z_scale = sb("z_scale", [P, FC], F32)
        one = sb("one", [P, 12], F32)
        x_amax, x_up, h_amax, h_up, y_scale, wo_top, wo_topr, wo_part, xm_part, hm_part = [
            one[:, n:n + 1] for n in range(10)]

        ARENA = 14700
        arena = sb("arena", [P, ARENA], F32)
        at = [0]

        def cut(n, words, shape):
            a = at[0]
            at[0] += n * words
            assert at[0] <= ARENA
            return [arena[:, a + k * words:a + (k + 1) * words].rearrange(shape[0], **shape[1]) for k in range(n)]

        PAIR = ("p (b d) -> p b d", dict(b=2))
        FOUR = ("p (c b l) -> p c b l", dict(c=2, b=2))
        xin = cut(UNROLL, 512, PAIR)
        cin = cut(2, 512, PAIR)
        cturn = cut(1, 512, ("p (c k) -> p c k", dict(c=2)))[0]
        xn = cut(1, 512, PAIR)[0]
        x1 = cut(1, 512, PAIR)[0]
        xn1 = cut(1, 512, PAIR)[0]
        HALVES = ("p (s k) -> p s k", dict(s=2))
        cf16 = cut(1, 512, HALVES)[0].bitcast(F16).rearrange("p s (c r k) -> p s c r k", c=2, r=2)
        fx16 = cut(1, 512, HALVES)[0].bitcast(F16).rearrange("p s (c r k) -> p s c r k", c=2, r=2)
        qs = cut(1, 768, ("p (r e) -> p r e", dict(r=3)))[0]
        prod = cut(1, 1024, ("p (k r e) -> p k r e", dict(k=2, r=2)))[0]
        csum = prod[:, :, 0, :]
        cs16 = cut(1, 512, HALVES)[0].bitcast(F16).rearrange("p s (k e) -> p s k e", k=2)
        ct16 = cut(1, 512, HALVES)[0].bitcast(F16).rearrange("p s (c k) -> p s c k", c=2)
        vt = cut(2, 512, FOUR)
        mt = cut(1, 512, FOUR)[0]
        ot16 = cut(1, 512, HALVES)[0].bitcast(F16).rearrange("p s (c b l) -> p s c b l", c=2, b=2)
        SMALL = ("p (g k) -> p g k", dict(g=4))
        top = cut(2, 32, SMALL)
        lag = [v.bitcast(U32) for v in cut(2, 32, SMALL)]
        ex = cut(2, 16, SMALL)
        head_dim = cut(1, 16, SMALL)[0]
        head_dim_i = head_dim.bitcast(I32)
        shift = cut(1, 16, SMALL)[0]
        ssum = cut(1, 4, ("p (g k) -> p g k", dict(g=4)))[0]
        rsum = cut(1, 4, ("p (g k) -> p g k", dict(g=4)))[0]
        hot = cut(1, 256, ("p (g r k) -> p g r k", dict(g=4, r=HD)))[0]
        ot32 = cut(1, 512, FOUR)[0]
        wmix = cut(1, 64, ("p (g r) -> p g r", dict(g=4)))[0]
        wrep = cut(1, 512, ("p (g r h) -> p g r h", dict(g=4, r=HD)))[0]
        st1 = cut(1, 12, PAIR)[0]
        st2 = cut(1, 12, PAIR)[0]
        mv1 = cut(2, 4, PAIR)
        mv2 = cut(2, 4, PAIR)
        rs1 = cut(2, 2, ("p (b d) -> p b d", dict(b=2)))
        rs2 = cut(2, 2, ("p (b d) -> p b d", dict(b=2)))
        nm1 = cut(2, 2, ("p (b d) -> p b d", dict(b=2)))
        nm2 = cut(2, 2, ("p (b d) -> p b d", dict(b=2)))
        half = cut(1, 2, ("p (b d) -> p b d", dict(b=2)))[0]
        raw = xnt[:, :, :, :, :].rearrange("p n c b l -> p (n c b l)")[:, PAIRS * 512 - 10240:PAIRS * 512]
        w_in_raw = raw[:, 0:2048].rearrange("p (c d) -> p c d", c=FC)
        w_out_raw = raw[:, 2048:4096].rearrange("p (c n) -> p c n", c=FC)
        w_in_i = raw[:, 4096:5120].bitcast(I16).rearrange("p (c d) -> p c d", c=FC)
        w_out_i = raw[:, 5120:6144].bitcast(I16).rearrange("p (c d) -> p c d", c=FC)
        w_in_qt = raw[:, 6144:8192].rearrange("p (c d) -> p c d", c=FC)
        w_attn_raw = raw[:, 8192:10240].rearrange("p (w c n) -> p w c n", w=4, c=DC)
        at = [0]
        hidden_in = cut(1, SAVED * 512, ("p (f t) -> p f t", dict(f=SAVED)))[0]
        xi = hidden_in[:, 0, :].bitcast(I16).rearrange("p (c n t) -> p c n t", c=2, n=2)
        hid = cut(2, 512, ("p (k) -> p k", {}))
        hq = [v.bitcast(I16) for v in cut(4, 256, ("p (k) -> p k", {}))]
        halls = cut(2, FC * 512, ("p (f t) -> p f t", dict(f=FC)))
        gbuf = [v.rearrange("p f t -> p (f t)").bitcast(F16).rearrange("p (s f t) -> p s f t", s=2, f=FC) for v in halls]
        yq = cut(1, 2048, ("p (m b d) -> p m b d", dict(m=2, b=4)))[0]

        bank = [ctx.enter_context(nc.psum_tensor(f"bank{n}", [P, 512], F32)) for n in range(8)]
        four = lambda n: bank[n][:, :].rearrange("p (c b l) -> p c b l", c=2, b=2)
        freq = lambda n: bank[n][:, :].rearrange("p (c r b f) -> p c r b f", c=2, r=2, b=2)
        pair = lambda n: bank[n][:, :].rearrange("p (b d) -> p b d", b=2)

        names = """const_in direct_in weights_in w_in_loaded ffn_in w_in_rounded w_in_back w_in_ready
            half_ready p1 p2 rstd1 rstd2 ln1 ln1_stats ln2_stats front_cf front_fx cf_out fx_out
            v_done k_done q_done vt_out q_out q_patched terms_done sums_done inv_done sc_top hd_done
            top_done shift_done exp_done w16_done wrep_done mt_done mt_out ot_done ot_out ot_low
            fx_low cf_low sum_high cs_ready ct_high ct_ready w_high w_split y_done x1_done xn1_done
            xnt_done xnt_out xmax_part x_chain w_chain ln_chain wo_chain sc_chain xmax_all x_scale
            wtop_all xi_done xhi_done xlo_done b_mm b_gelu b_max hmax_part hmax_all h_scale c_mm
            c_gelu c_hq c_hi c_lo c_y c_x1b c_out""".split()
        S = {n: sem("s_" + n) for n in names}
        s_x_in = [sem(f"s_x_in{n}") for n in range(UNROLL)]
        s_t_in = sem("s_t_in")
        s_c_in = [sem(f"s_c_in{n}") for n in range(2)]
        s_x1_st = sem("s_x1_st")
        s_x1_ld = [sem(f"s_x1_ld{n}") for n in range(2)]
        s_h_st = [sem(f"s_h_st{n}") for n in range(2)]
        s_h_ld = sem("s_h_ld")
        s_out = [sem(f"s_out{n}") for n in range(2)]

        def wait(eng, s, n):
            if isinstance(n, int) and n <= 0:
                return
            eng.wait_ge(s, n)

        def upto(n):
            return min(n, PAIRS) if isinstance(n, int) else n

        s_passed = sem("s_passed")

        def wait_apart(eng, s, n):
            eng.wait_ge(s, n)
            if not isinstance(n, int):
                eng.sem_inc(s_passed, 1)

        def steps(eng, step, last=LAST):
            for t in range(PEELED):
                step(t, t % UNROLL)
            with eng.Fori(PEELED // UNROLL, PAIRS // UNROLL) as j:
                for k in range(UNROLL):
                    step(j * UNROLL + k, k)
            for t in range(PAIRS, PAIRS + last):
                step(t, t % UNROLL)

        def mixing_bank(p):
            return 1 + p % 2 if isinstance(p, int) and p > PAIRS - 4 else 0

        def active(t, lagged):
            if isinstance(t, int):
                return 0 <= t - lagged < PAIRS
            return True

        def landed(t, n):
            return 16 * (t // 2 + 1) if isinstance(t, int) else (t - n % 2) * 8 + 16

        NEW = FC - SAVED
        block = ctx.enter_context(nc.Block())

        @block.sync
        def _(sp):
            sp.dma_start(w_in_raw, w_in.rearrange("(c p) d -> p c d", p=P)).then_inc(S["w_in_loaded"], 16)
            sp.dma_start(cst[:, :], table).then_inc(S["const_in"], 16)

            def rows(v, p):
                if isinstance(p, int):
                    return v[p]
                names = "abcde"[:len(v.shape) - 1]
                return v[(bass.ds(p, 1),) + (slice(None),) * (len(v.shape) - 1)].rearrange(
                    f"n {' '.join(names)} -> (n {names[0]}) {' '.join(names[1:])}")

            def load_x(t, n):
                wait(sp, S["x1_done"], t - (UNROLL - 1))
                sp.dma_start(xin[n], rows(x_v, t)).then_inc(s_x_in[n], 16)

            def load_context(t, n):
                wait(sp, S["front_cf"], t - 1)
                sp.dma_start(cin[n % 2], rows(c_v, t)).then_inc(s_c_in[n % 2], 16)

            def load_turned(p):
                wait(sp, S["ct_ready"], p)
                sp.dma_start(cturn, rows(ctx_turned, p)).then_inc(s_t_in, 16)

            load_x(0, 0)
            for n, w in enumerate((wq, wv, wo, wk)):
                sp.dma_start(w_attn_raw[:, n, :, :], w.rearrange("(c p) n -> p c n", p=P)).then_inc(S["weights_in"], 16)
            load_context(0, 0)
            sp.dma_start(w_out_raw, w_out.rearrange("(c p) n -> p c n", p=P)).then_inc(S["ffn_in"], 16)
            sp.dma_start(inv16[:, :, :, :], inv_table).then_inc(S["direct_in"], 16)
            load_x(1, 1)
            load_context(1, 1)
            sp.dma_start(b_in_sb[:, :], b_in.rearrange("(c p) -> p c", p=P), allow_slow_non_contiguous=True).then_inc(S["ffn_in"], 16)
            sp.dma_start(b_out_sb[:, :], b_out.rearrange("(a n) -> a n", a=1).broadcast_to([P, D])).then_inc(S["ffn_in"], 16)

            def step(t, n):
                if active(t, 0) and not (isinstance(t, int) and t < 2):
                    load_x(t, n)
                if active(t, 1) and not (isinstance(t, int) and t < 3):
                    load_context(t - 1, n - 1)
                if active(t, LAST + 1):
                    p = t - (LAST + 1)
                    wait(sp, S["x1_done"], p + 1)
                    sp.dma_start(rows(x1_v, p), x1).then_inc(s_x1_st, 16)
                if active(t, 2):
                    load_turned(t - 2)

            steps(sp, step, LAST + 1)
            sp.wait_ge(s_x1_st, 16 * PAIRS)
            def store_hidden(q, m):
                sp.wait_ge(S["b_gelu"], q * FC + (FC + SAVED))
                sp.dma_start(rows(h_dram, q), halls[m][:, 0:SAVED, :].rearrange("p f t -> p (f t)")).then_inc(s_h_st[m], 16)

            with sp.Fori(0, QUADS // 2) as i:
                for m in range(2):
                    store_hidden(i * 2 + m, m)
            sp.wait_ge(s_h_st[0], 16 * (QUADS // 2))

            def load_hidden(q):
                wait(sp, S["c_hq"], (q - 1) * FC + SAVED)
                sp.dma_start(hidden_in.rearrange("p f t -> p (f t)"), rows(h_dram, q)).then_inc(s_h_ld, 16)

            def load_x1(q, m):
                wait(sp, s_out[m], 16 * ((q - m) // 2) if isinstance(q, int) else (q - m) * 8)
                sp.dma_start(yq[:, m, :, :], rows(x1_q, q)).then_inc(s_x1_ld[m], 16)

            def store(q, m):
                wait(sp, S["c_out"], (q + 1) * 4)
                sp.dma_start(rows(out_q, q), yq[:, m, :, :]).then_inc(s_out[m], 16)

            sp.wait_ge(S["xlo_done"], QUADS)
            load_hidden(0)
            load_x1(0, 0)
            load_x1(1, 1)
            sp.wait_ge(s_h_st[1], 16 * (QUADS // 2))
            load_hidden(1)
            with sp.Fori(0, QUADS // 2 - 1) as i:
                for m in range(2):
                    load_hidden(i * 2 + (m + 2))
                    store(i * 2 + m, m)
                    load_x1(i * 2 + (m + 2), m)
            store(QUADS - 2, 0)
            store(QUADS - 1, 1)
            for m in range(2):
                sp.wait_ge(s_out[m], 16 * (QUADS // 2))

        @block.tensor
        def _(pe):
            pe.wait_ge(S["const_in"], 16)
            pe.wait_ge(S["w_in_rounded"], 1)
            for f in range(FC):
                for c in range(DC):
                    last = nc.tensor.transpose(bank[f][:, c * P:(c + 1) * P], w_in_qt[:, f, c * P:(c + 1) * P], ident)
                last.then_inc(S["w_in_back"], 1)
            pe.wait_ge(S["direct_in"], 16)
            pe.wait_ge(S["w_split"], 1)
            pe.wait_ge(S["w_in_ready"], 2)

            PARTS = ((0, 0), (1, 0), (0, 1))

            def dft_context(p, n):
                m = n % 2
                wait(pe, s_c_in[m], landed(p, n))
                wait(pe, S["cf_low"], p)
                for c in range(DC):
                    for b in range(2):
                        last = nc.tensor.matmul(freq(1)[:, c, :, b, :], cin[m][:, b, c * P:(c + 1) * P], dft, start=True, stop=True)
                last.then_inc(S["front_cf"], 1)

            def dft_norm(p, n):
                m = n % 2
                wait(pe, S["ln1"], p + 1)
                wait(pe, S["fx_low"], p)
                for c in range(DC):
                    for b in range(2):
                        last = nc.tensor.matmul(freq(2)[:, c, :, b, :], xn[:, b, c * P:(c + 1) * P], dft, start=True, stop=True)
                last.then_inc(S["front_fx"], 1)

            def project_k(p):
                wait(pe, S["cf_low"], p + 1)
                wait(pe, S["terms_done"], p)
                for r in range(2):
                    for c in range(DC):
                        for n, (i, j) in enumerate(PARTS):
                            last = nc.tensor.matmul(bank[3][:, r * D:(r + 1) * D], cf16[:, i, c, r, :], w16[:, j, 3, c, :],
                                                    start=c == 0 and n == 0, stop=c == DC - 1 and n == 2)
                last.then_inc(S["k_done"], 1)

            def project_q(p):
                wait(pe, S["fx_low"], p + 1)
                wait(pe, S["q_patched"], p)
                for r in range(2):
                    for c in range(DC):
                        for n, (i, j) in enumerate(PARTS):
                            last = nc.tensor.matmul(bank[4][:, r * D:(r + 1) * D], fx16[:, i, c, r, :], w16[:, j, 0, c, :],
                                                    start=c == 0 and n == 0, stop=c == DC - 1 and n == 2)
                last.then_inc(S["q_done"], 1)

            def project_v(p, n):
                wait(pe, S["ct_ready"], p + 1)
                wait(pe, S["vt_out"], p)
                for e in range(DC):
                    for c in range(DC):
                        for k, (i, j) in enumerate(PARTS):
                            last = nc.tensor.matmul(bank[6][:, e * D:(e + 1) * D], w16[:, j, 1, c, e * P:(e + 1) * P],
                                                    ct16[:, i, c, :], start=c == 0 and k == 0, stop=c == DC - 1 and k == 2)
                last.then_inc(S["v_done"], 1)

            def mixing(p):
                wait(pe, S["wrep_done"], p + 1)
                if mixing_bank(p) == 0:
                    wait(pe, S["x1_done"], p)
                for c in range(DC):
                    for b in range(2):
                        last = nc.tensor.transpose(four(mixing_bank(p))[:, c, b, :], wrep[:, 2 * c + b, :, :].rearrange("p r h -> p (r h)"), ident)
                last.then_inc(S["mt_done"], 1)

            def turn_ln2(p, n):
                wait(pe, S["xn1_done"], p + 1)
                wait(pe, S["ot_out"], upto(p + 2))
                for c in range(DC):
                    for b in range(2):
                        last = nc.tensor.transpose(four(7)[:, c, b, :], xn1[:, b, c * P:(c + 1) * P], ident)
                last.then_inc(S["xnt_done"], 1)

            def attend(p, n):
                wait(pe, S["mt_out"], p + 1)
                wait(pe, S["vt_out"], p + 1)
                wait(pe, S["xnt_out"], p - 1)
                for c in range(DC):
                    for b in range(2):
                        last = nc.tensor.matmul(four(7)[:, c, b, :], vt[n % 2][:, c, b, :], mt[:, c, b, :], start=True, stop=True)
                last.then_inc(S["ot_done"], 1)

            def project_out(p):
                wait(pe, S["ot_low"], p + 1)
                wait(pe, S["mt_out"], p + 1)
                if mixing_bank(p) != 0:
                    wait(pe, S["x1_done"], p)
                for b in range(2):
                    for c in range(DC):
                        for n, (i, j) in enumerate(PARTS):
                            last = nc.tensor.matmul(pair(0)[:, b, :], ot16[:, i, c, b, :], w16[:, j, 2, c, :],
                                                    start=c == 0 and n == 0, stop=c == DC - 1 and n == 2)
                last.then_inc(S["y_done"], 1)

            def inverse(p):
                wait(pe, S["cs_ready"], p + 1)
                wait(pe, S["top_done"], p)
                for e in range(DC):
                    for k in range(2):
                        for n, (i, j) in enumerate(PARTS):
                            last = nc.tensor.matmul(bank[5][:, e * D:(e + 1) * D], cs16[:, i, k, e * P:(e + 1) * P],
                                                    inv16[:, j, k, :], start=k == 0 and n == 0, stop=k == 1 and n == 2)
                last.then_inc(S["inv_done"], 1)

            def step(t, n):
                if active(t, 1):
                    dft_context(t - 1, n - 1)
                if active(t, 5):
                    project_out(t - 5)
                if active(t, 1):
                    dft_norm(t - 1, n - 1)
                if active(t, 3):
                    project_v(t - 3, n - 3)
                if active(t, 4):
                    mixing(t - 4)
                if active(t, 1):
                    project_q(t - 1)
                if active(t, 4):
                    attend(t - 4, n - 4)
                if active(t, 2):
                    inverse(t - 2)
                if active(t, 1):
                    project_k(t - 1)
                if active(t, 5):
                    turn_ln2(t - 5, n - 5)

            steps(pe, step)

            pe.wait_ge(S["top_done"], PAIRS)
            pe.wait_ge(S["x1_done"], PAIRS)
            pe.wait_ge(S["xnt_out"], PAIRS)

            def hidden(q, f, b):
                for s in range(2):
                    for c in range(DC):
                        rhs = xq[:, bass.ds(q, 1), s, c, :].rearrange("p q t -> p (q t)")
                        last = nc.tensor.matmul(bank[b][:, :], win16[:, c, f * P:(f + 1) * P], rhs,
                                                start=s == 0 and c == 0, stop=s == 1 and c == DC - 1)
                return last

            with pe.Fori(0, QUADS) as q:
                pe.wait_ge(S["xlo_done"], q + 1)
                for f in range(FC):
                    pe.wait_ge(S["b_gelu"], q * FC + (f + 1))
                    hidden(q, f, f).then_inc(S["b_mm"], 1)

            pe.wait_ge(S["b_gelu"], (QUADS + 1) * FC)

            def output(q, m, tchunk):
                wait(pe, S["c_out"], (q - 1) * 4 + (tchunk + 1))
                for f in range(FC):
                    wait(pe, S["c_lo"], q * FC + (f + 1))
                    for s in range(2):
                        last = nc.tensor.matmul(bank[4 + tchunk][:, 0:D], gbuf[m][:, s, f, tchunk * P:(tchunk + 1) * P],
                                                wout16[:, f, :], start=f == 0 and s == 0, stop=f == FC - 1 and s == 1)
                last.then_inc(S["c_y"], 1)

            def last_in_bank(k):
                return max(n for n in range(NEW) if n % 4 == k % 4)

            def quad(q, m, has_hidden, has_output):
                for f in range(SAVED, FC):
                    k = f - SAVED
                    if has_hidden:
                        wait(pe, S["c_gelu"], q * NEW + (k - 3) if k > 3 else (q - 1) * NEW + (last_in_bank(k) + 1))
                        hidden(q, f, k % 4).then_inc(S["c_mm"], 1)
                    for tchunk in range(4):
                        if has_output and f == OUT_AFTER[tchunk]:
                            output(q - 1, 1 - m, tchunk)

            quad(0, 0, True, False)
            quad(1, 1, True, True)
            with pe.Fori(1, QUADS // 2) as i:
                quad(i * 2, 0, True, True)
                quad(i * 2 + 1, 1, True, True)
            quad(QUADS, 0, False, True)

        @block.scalar
        def _(act):
            def copy(dst, src, done):
                nc.scalar.activation(dst, src, ACT.Copy).then_inc(S[done], 1)

            act.wait_ge(S["weights_in"], 64)
            nc.scalar.activation(w16[:, 0], w_attn_raw, ACT.Copy, scale=W_UP).then_inc(S["w_high"], 1)
            for f in range(FC // 2):
                act.wait_ge(S["w_in_back"], f + 1)
                last = nc.scalar.activation(win16[:, :, f * P:(f + 1) * P], bank[f][:, 0:D].rearrange("p (c e) -> p c e", c=DC), ACT.Copy)
            last.then_inc(S["w_in_ready"], 1)
            act.wait_ge(S["w_in_ready"], 2)

            def normalize(dst, src, rs, nm, done):
                for b in range(2):
                    last = nc.scalar.activation(dst[:, b, :], src[:, b, :], ACT.Identity, bias=nm[:, b, :], scale=rs[:, b, :])
                last.then_inc(S[done], 1)

            def step(t, n):
                if active(t, 3):
                    p, m = t - 3, (n - 3) % 2
                    act.wait_ge(S["shift_done"], p + 1)
                    wait(act, S["w16_done"], p - 1)
                    nc.scalar.activation(ex[m], shift, ACT.Exp, scale=1.0 / CORR_UP).then_inc(S["exp_done"], 1)
                if active(t, 1):
                    p = t - 1
                    act.wait_ge(S["front_cf"], p + 1)
                    wait(act, S["k_done"], p)
                    copy(cf16[:, 0].rearrange("p c r k -> p (c r k)"), bank[1][:, :], "cf_out")
                    act.wait_ge(S["front_fx"], p + 1)
                    wait(act, S["q_done"], p)
                    copy(fx16[:, 0].rearrange("p c r k -> p (c r k)"), bank[2][:, :], "fx_out")
                if active(t, 2):
                    p = t - 2
                    act.wait_ge(S["sums_done"], p + 1)
                    wait(act, S["inv_done"], p)
                    copy(cs16[:, 0], csum, "sum_high")
                if active(t, 3):
                    p, m = t - 3, (n - 3) % 2
                    act.wait_ge(S["v_done"], p + 1)
                    wait(act, S["ot_done"], p - 1)
                    nc.scalar.activation(vt[m].rearrange("p c b l -> p (c b l)"), bank[6][:, :], ACT.Copy, scale=1.0 / W_UP).then_inc(S["vt_out"], 1)
                if active(t, 2):
                    p = t - 2
                    wait(act, s_t_in, p * 16 + 16)
                    wait(act, S["v_done"], p)
                    copy(ct16[:, 0], cturn, "ct_high")
                if active(t, 1):
                    p = t - 1
                    act.wait_ge(S["q_done"], p + 1)
                    wait(act, S["terms_done"], p)
                    nc.scalar.activation(qs[:, 0, :], bank[4][:, 0:D], ACT.Copy, scale=Q_DOWN)
                    nc.scalar.activation(qs[:, 1, :], bank[4][:, D:2 * D], ACT.Copy, scale=keep)
                    nc.scalar.activation(qs[:, 2, :], bank[4][:, 0:D], ACT.Copy, scale=minus_keep).then_inc(S["q_out"], 1)
                if active(t, 5):
                    p, m = t - 5, (n - 5) % 2
                    act.wait_ge(S["rstd2"], p + 1)
                    wait(act, S["xmax_part"], p)
                    wait(act, S["xnt_done"], p)
                    normalize(xn1, x1, rs2[m], nm2[m], "xn1_done")
                if active(t, 4):
                    p = t - 4
                    act.wait_ge(S["ot_done"], p + 1)
                    wait(act, S["y_done"], p)
                    nc.scalar.activation(ot16[:, 0].rearrange("p c b l -> p (c b l)"), bank[7][:, :], ACT.Copy)
                    wait(act, S["ot_low"], p)
                    copy(ot32.rearrange("p c b l -> p (c b l)"), bank[7][:, :], "ot_out")
                if active(t, 3):
                    p = t - 3
                    act.wait_ge(S["w16_done"], p + 1)
                    wait(act, S["mt_done"], p)
                    copy(wrep, wmix.unsqueeze(3).broadcast_to([P, 4, HD, NH]), "wrep_done")
                if active(t, 0):
                    act.wait_ge(S["rstd1"], t + 1)
                    wait(act, S["front_fx"], t)
                    normalize(xn, xin[n], rs1[n % 2], nm1[n % 2], "ln1")
                if active(t, 5):
                    p = t - 5
                    act.wait_ge(S["xnt_done"], p + 1)
                    dst = xnt[:, p, :, :, :] if isinstance(p, int) else xnt[:, bass.ds(p, 1), :, :, :].rearrange("p n c b l -> p (n c) b l")
                    copy(dst, four(7), "xnt_out")

            steps(act, step)

            act.wait_ge(S["x_scale"], 1)

            def gelu(dst, b, f, done):
                nc.scalar.activation(dst, bank[b][:, :], ACT.Gelu, bias=b_in_sb[:, f:f + 1],
                                     scale=z_scale[:, f:f + 1]).then_inc(S[done], 1)

            act.nop().then_inc(S["b_gelu"], FC)

            def first(q, m):
                for f in range(FC):
                    act.wait_ge(S["b_mm"], q * FC + (f + 1))
                    wait(act, S["b_max"], (q - 2) * FC + (f + 1))
                    if f == 0:
                        wait(act, s_h_st[m], 16 * ((q - m) // 2) if isinstance(q, int) else (q - m) * 8)
                    gelu(halls[m][:, f, :], f, f, "b_gelu")

            first(0, 0)
            first(1, 1)
            with act.Fori(1, QUADS // 2) as i:
                first(i * 2, 0)
                first(i * 2 + 1, 1)

            act.wait_ge(S["h_scale"], 1)

            def to_int(q, f, src):
                wait(act, S["c_lo"], q * FC + (f - 3))
                nc.scalar.activation(hq[f % 4], src, ACT.Copy, scale=h_up).then_inc(S["c_hq"], 1)

            def quad(q, m):
                act.wait_ge(s_h_ld, q * 16 + 16)
                for f in range(SAVED):
                    to_int(q, f, hidden_in[:, f, :])
                for f in range(SAVED, FC):
                    k = f - SAVED
                    act.wait_ge(S["c_mm"], q * NEW + (k + 1))
                    wait(act, S["c_hq"], q * FC + (f - 1) if k > 1 else (q - 1) * FC + (FC - 1 + k))
                    gelu(hid[(m * NEW + k) % 2], k % 4, f, "c_gelu")
                    if k > 0:
                        act.wait_ge(S["c_gelu"], q * NEW + k)
                        to_int(q, f - 1, hid[(m * NEW + k - 1) % 2])
                act.wait_ge(S["c_gelu"], q * NEW + NEW)
                to_int(q, FC - 1, hid[(m * NEW + NEW - 1) % 2])

            quad(0, 0)
            quad(1, 1)
            with act.Fori(1, QUADS // 2) as i:
                quad(i * 2, 0)
                quad(i * 2 + 1, 1)

        @block.gpsimd
        def _(pool):
            pool.wait_ge(S["w_in_ready"], 2)
            nc.gpsimd.memset(half, -0.5).then_inc(S["half_ready"], 1)
            pool.wait_ge(S["half_ready"], 1)

            def rstd(p, m, mv, rs, nm, stats, chain, taken, done):
                pool.wait_ge(S[stats], p + 1)
                wait_apart(pool, S[stats], p + 1)
                if not isinstance(p, int) or p > 1:
                    wait_apart(pool, S[taken], p - 1)
                nc.gpsimd.tensor_scalar(nm[m], mv[m][:, :, 0:1], -1.0, None, ALU.mult)
                nc.gpsimd.tensor_scalar(rs[m], mv[m][:, :, 1:2], EPS, None, ALU.add).then_inc(S[chain], 1)
                pool.wait_ge(S[chain], p * 2 + 1)
                nc.gpsimd.tensor_tensor(rs[m], rs[m], half, ALU.pow).then_inc(S[chain], 1)
                pool.wait_ge(S[chain], p * 2 + 2)
                nc.gpsimd.tensor_tensor(nm[m], nm[m], rs[m], ALU.mult).then_inc(S[done], 1)

            def step(t, n):
                if active(t, 2):
                    p = t - 2
                    pool.wait_ge(S["terms_done"], p + 1)
                    wait(pool, S["cs_ready"], p)
                    nc.gpsimd.tensor_tensor(csum, prod[:, :, 0, :], prod[:, :, 1, :], ALU.add).then_inc(S["sums_done"], 1)
                if active(t, 2):
                    p = t - 2
                    pool.wait_ge(S["sum_high"], p + 1)
                    nc.gpsimd.tensor_tensor(cs16[:, 1], csum, cs16[:, 0], ALU.subtract).then_inc(S["cs_ready"], 1)
                if active(t, 5):
                    rstd(t - 5, (n - 5) % 2, mv2, rs2, nm2, "ln2_stats", "p2", "xn1_done", "rstd2")
                if active(t, 0):
                    rstd(t, n % 2, mv1, rs1, nm1, "ln1_stats", "p1", "ln1", "rstd1")
                if active(t, 4):
                    pool.wait_ge(S["ot_out"], t - 4 + 1)
                    nc.gpsimd.tensor_tensor(ot16[:, 1], ot32, ot16[:, 0], ALU.subtract).then_inc(S["ot_low"], 1)
                if active(t, 2):
                    p = t - 2
                    pool.wait_ge(S["ct_high"], p + 1)
                    nc.gpsimd.tensor_tensor(ct16[:, 1], cturn, ct16[:, 0], ALU.subtract).then_inc(S["ct_ready"], 1)

                if isinstance(t, int) and t == 1:
                    pool.wait_ge(S["wo_chain"], 1)
                    nc.gpsimd.partition_all_reduce(wo_top, wo_part, P, RMAX).then_inc(S["wtop_all"], 1)

            steps(pool, step)
            pool.wait_ge(S["sc_chain"], 3)
            nc.gpsimd.partition_all_reduce(x_amax, xm_part, P, RMAX).then_inc(S["xmax_all"], 1)
            pool.wait_ge(S["hmax_part"], 1)
            nc.gpsimd.partition_all_reduce(h_amax, hm_part, P, RMAX).then_inc(S["hmax_all"], 1)
            def bias(q, m):
                wait(pool, s_x1_ld[m], 16 * ((q - m) // 2 + 1) if isinstance(q, int) else (q - m) * 8 + 16)
                nc.gpsimd.tensor_tensor(yq[:, m, :, :], yq[:, m, :, :], b_out_sb[:, :].unsqueeze(1).broadcast_to([P, 4, D]),
                                        ALU.add).then_inc(S["c_x1b"], 1)
            with pool.Fori(0, QUADS // 2) as i:
                bias(i * 2, 0)
                bias(i * 2 + 1, 1)

        @block.vector
        def _(dve):
            V = nc.vector
            chain = [0]

            def link(ins):
                chain[0] += 1
                ins.then_inc(S["w_chain"], 1)
                dve.wait_ge(S["w_chain"], chain[0])

            def round_rows(raw, top_, up, ints):
                link(V.tensor_reduce(top_[:, :], raw, AX_X, ALU.max, apply_absolute_value=True))
                link(V.tensor_scalar(top_[:, :], top_[:, :], TINY, None, ALU.max))
                link(V.reciprocal(up[:, :], top_[:, :]))
                link(V.tensor_scalar(up[:, :], up[:, :], INT8, None, ALU.mult))
                link(V.tensor_tensor(ints, raw, up[:, :].unsqueeze(2).broadcast_to([P, FC, D]), ALU.mult))

            dve.wait_ge(S["w_in_loaded"], 16)
            round_rows(w_in_raw, win_max, win_up, w_in_i)
            V.tensor_copy(w_in_qt, w_in_i).then_inc(S["w_in_rounded"], 1)
            dve.wait_ge(S["w_high"], 1)
            flat = lambda v: v.rearrange("p w c n -> p (w c n)")
            V.scalar_tensor_tensor(flat(w16[:, 1]), flat(w_attn_raw), W_UP, flat(w16[:, 0]), ALU.mult, ALU.subtract).then_inc(S["w_split"], 1)
            for f in range(FC // 2, FC):
                dve.wait_ge(S["w_in_back"], f + 1)
                last = V.tensor_copy(win16[:, :, f * P:(f + 1) * P], bank[f][:, 0:D].rearrange("p (c e) -> p c e", c=DC))
            last.then_inc(S["w_in_ready"], 1)
            dve.wait_ge(S["w_in_ready"], 2)

            def round_w_out(part):
                if part == 0:
                    dve.wait_ge(S["ffn_in"], 48)
                    link(V.tensor_reduce(wout_max[:, :], w_out_raw, AX_X, ALU.max, apply_absolute_value=True))
                elif part == 1:
                    link(V.tensor_scalar(wout_max[:, :], wout_max[:, :], TINY, None, ALU.max))
                    link(V.reciprocal(wout_up[:, :], wout_max[:, :]))
                    link(V.tensor_scalar(wout_up[:, :], wout_up[:, :], INT8, None, ALU.mult))
                    V.tensor_reduce(wo_part, wout_max[:, :], AX_X, ALU.max).then_inc(S["wo_chain"], 1)
                elif part == 2:
                    link(V.tensor_tensor(w_out_i, w_out_raw, wout_up[:, :].unsqueeze(2).broadcast_to([P, FC, D]), ALU.mult))
                else:
                    link(V.tensor_copy(wout16[:, :, :], w_out_i))

            def statistics1(t, n):
                wait(dve, s_x_in[n], 16 * (t // UNROLL + 1) if isinstance(t, int) else (t - n) * (16 // UNROLL) + 16)
                wait(dve, S["ln1_stats"], t)
                for b in range(2):
                    last = V.bn_stats(st1[:, b, :], xin[n][:, b, :])
                last.then_inc(S["ln_chain"], 1)

            def moments1(t, n):
                m = n % 2
                wait_apart(dve, S["ln_chain"], t + 1)
                if not isinstance(t, int) or t > 1:
                    wait_apart(dve, S["rstd1"], t - 1)
                for b in range(2):
                    last = V.bn_aggr(mv1[m][:, b, :], st1[:, b, :])
                last.then_inc(S["ln1_stats"], 1)

            def spread(p, n):
                m = n % 2
                dve.wait_ge(S["hd_done"], p + 1)
                V.tensor_tensor(hot, cst[:, C_IOTA:C_IOTA + HD].unsqueeze(1).unsqueeze(3).broadcast_to([P, 4, HD, KTOP]),
                                head_dim_i.unsqueeze(2).broadcast_to([P, 4, HD, KTOP]), ALU.is_equal).then_inc(S["w_chain"], 1)
                dve.wait_ge(S["exp_done"], p + 1)
                V.tensor_reduce(ssum[:, :, 0:1], ex[m], AX_X, ALU.add).then_inc(S["w_chain"], 1)

            def select(p, n):
                m = n % 2
                dve.wait_ge(S["w_chain"], p * 5 + (chain[0] + 1))
                V.tensor_tensor(hot, hot, ex[m].unsqueeze(2).broadcast_to([P, 4, HD, KTOP]), ALU.mult).then_inc(S["w_chain"], 1)
                dve.wait_ge(S["w_chain"], p * 5 + (chain[0] + 2))
                V.reciprocal(rsum[:, :, 0:1], ssum[:, :, 0:1]).then_inc(S["w_chain"], 1)
                dve.wait_ge(S["w_chain"], p * 5 + (chain[0] + 3))
                wait(dve, S["wrep_done"], p)
                V.tensor_reduce(wmix, hot, AX_X, ALU.add).then_inc(S["w_chain"], 1)

            def weigh(p):
                dve.wait_ge(S["w_chain"], p * 5 + (chain[0] + 5))
                V.tensor_tensor(wmix, wmix, rsum[:, :, 0:1].broadcast_to([P, 4, HD]), ALU.mult).then_inc(S["w16_done"], 1)

            def mix_out(p):
                dve.wait_ge(S["mt_done"], p + 1)
                wait(dve, S["ot_done"], p)
                V.tensor_tensor(mt.rearrange("p c b l -> p (c b) l"), four(mixing_bank(p)).rearrange("p c b l -> p (c b) l"),
                                mask.unsqueeze(1).broadcast_to([P, 4, P]), ALU.mult).then_inc(S["mt_out"], 1)

            def take_low(dst, src, high, ready, done, p):
                dve.wait_ge(S[ready], p + 1)
                V.tensor_tensor(dst, src, high, ALU.subtract).then_inc(S[done], 1)

            def patch_q(p):
                dve.wait_ge(S["q_out"], p + 1)
                V.scalar_tensor_tensor(qs[:, 2, :], bank[4][:, D:2 * D], drop, qs[:, 2, :], ALU.mult, ALU.add).then_inc(S["q_patched"], 1)

            def products(p):
                dve.wait_ge(S["k_done"], p + 1)
                wait(dve, S["cs_ready"], p)
                ps = bank[3][:, :].rearrange("p (r e) -> p r e", r=2)
                V.tensor_tensor(prod[:, 0, :, :], qs[:, 0:2, :], ps, ALU.mult)
                dve.wait_ge(S["q_patched"], p + 1)
                V.tensor_tensor(prod[:, 1, :, :], qs[:, 1:3, :], ps, ALU.mult).then_inc(S["terms_done"], 1)

            def residual(p, n):
                dve.wait_ge(S["y_done"], p + 1)
                wait(dve, s_x1_st, p * 16)
                wait(dve, S["xn1_done"], p)
                V.scalar_tensor_tensor(x1, pair(0), 1.0 / W_UP, xin[n], ALU.mult, ALU.add).then_inc(S["x1_done"], 1)

            def statistics2(p):
                dve.wait_ge(S["x1_done"], p + 1)
                wait(dve, S["ln2_stats"], p)
                for b in range(2):
                    last = V.bn_stats(st2[:, b, :], x1[:, b, :])
                last.then_inc(S["x_chain"], 1)

            def moments2(p, n):
                m = n % 2
                wait_apart(dve, S["x_chain"], p + 1)
                if not isinstance(p, int) or p > 1:
                    wait_apart(dve, S["rstd2"], p - 1)
                for b in range(2):
                    last = V.bn_aggr(mv2[m][:, b, :], st2[:, b, :])
                last.then_inc(S["ln2_stats"], 1)

            def magnitude(p, n):
                wait_apart(dve, S["xn1_done"], p + 1)
                V.tensor_reduce(xmax[:, bass.ds(p, 1)], xn1, AX_XY, ALU.max, apply_absolute_value=True).then_inc(S["xmax_part"], 1)

            def top_values(p, n):
                m = n % 2
                wait_apart(dve, S["inv_done"], p + 1)
                for g in range(4):
                    last = V.max(top[m][:, g, :], four(5)[:, g // 2, g % 2, :])
                last.then_inc(S["sc_top"], 1)

            def top_places(p, n):
                m = n % 2
                dve.wait_ge(S["sc_top"], p * 2 + 1)
                wait(dve, S["exp_done"], p)
                V.tensor_tensor(shift, top[m][:, :, 0:KTOP], top[m][:, :, 0:1].broadcast_to([P, 4, KTOP]), ALU.subtract).then_inc(S["shift_done"], 1)
                for g in range(4):
                    last = V.max_index(lag[m][:, g, :], top[m][:, g, :], four(5)[:, g // 2, g % 2, :])
                last.then_inc(S["top_done"], 1)

            def negate_lags(p, n):
                m = n % 2
                dve.wait_ge(S["top_done"], p + 1)
                V.scalar_tensor_tensor(head_dim_i, lag[m][:, :, 0:KTOP], -1.0, low.unsqueeze(1).broadcast_to([P, 4, KTOP]),
                                       ALU.mult, ALU.add).then_inc(S["sc_top"], 1)

            def head_lags(p):
                dve.wait_ge(S["sc_top"], p * 2 + 2)
                V.tensor_scalar(head_dim_i, head_dim_i, HD - 1, None, ALU.bitwise_and).then_inc(S["hd_done"], 1)


            def step(t, n):
                if active(t, 1):
                    take_low(cf16[:, 1].rearrange("p c r k -> p (c r k)"), bank[1][:, :],
                             cf16[:, 0].rearrange("p c r k -> p (c r k)"), "cf_out", "cf_low", t - 1)
                if isinstance(t, int) and t == 1:
                    round_w_out(1)
                if active(t, 5):
                    residual(t - 5, (n - 5) % UNROLL)
                if active(t, 3):
                    head_lags(t - 3)
                if active(t, 5):
                    statistics2(t - 5)
                if active(t, 1):
                    take_low(fx16[:, 1].rearrange("p c r k -> p (c r k)"), bank[2][:, :],
                             fx16[:, 0].rearrange("p c r k -> p (c r k)"), "fx_out", "fx_low", t - 1)
                if active(t, 5):
                    moments2(t - 5, n - 5)
                if active(t, 4):
                    mix_out(t - 4)
                if active(t, 3):
                    spread(t - 3, n - 3)
                if active(t, 0):
                    statistics1(t, n)
                if active(t, 3):
                    select(t - 3, n - 3)
                if active(t, 0):
                    moments1(t, n)
                if isinstance(t, int) and t == 0:
                    round_w_out(0)
                if active(t, 3):
                    weigh(t - 3)
                if active(t, 1):
                    if isinstance(t, int) and t == 1:
                        round_w_out(2)
                    patch_q(t - 1)
                    if isinstance(t, int) and t == 2:
                        round_w_out(3)
                if active(t, 2):
                    top_values(t - 2, n - 2)
                if active(t, 5):
                    magnitude(t - 5, n - 5)
                if active(t, 2):
                    top_places(t - 2, n - 2)
                if active(t, 1):
                    products(t - 1)
                if active(t, 2):
                    negate_lags(t - 2, n - 2)

            steps(dve, step)

            sc = [0]

            def then(ins):
                sc[0] += 1
                ins.then_inc(S["sc_chain"], 1)
                dve.wait_ge(S["sc_chain"], sc[0])

            dve.wait_ge(S["wtop_all"], 1)
            then(V.reciprocal(wo_topr, wo_top))
            then(V.tensor_scalar(wout_rel[:, :], wout_max[:, :], wo_topr, None, ALU.mult))
            dve.wait_ge(s_x1_st, 16 * PAIRS)
            dve.wait_ge(S["xmax_part"], PAIRS)
            then(V.tensor_reduce(xm_part, xmax[:, :], AX_X, ALU.max))
            dve.wait_ge(S["xmax_all"], 1)
            then(V.tensor_scalar(x_amax, x_amax, TINY, None, ALU.max))
            then(V.reciprocal(x_up, x_amax))
            then(V.tensor_scalar(x_up, x_up, INT16, None, ALU.mult))
            then(V.tensor_scalar(z_scale[:, :], win_max[:, :], x_amax, 1.0 / INT8, ALU.mult, ALU.mult))
            V.tensor_scalar(z_scale[:, :], z_scale[:, :], 1.0 / INT16, None, ALU.mult).then_inc(S["x_scale"], 1)

            def round_x(q):
                src = xnt[:, bass.ds(q * 2, 2), :, :, :].rearrange("p n c b l -> p c n (b l)")
                wait(dve, S["xlo_done"], q)
                V.tensor_scalar(xi, src, x_up, None, ALU.mult).then_inc(S["xi_done"], 1)
                dve.wait_ge(S["xi_done"], q + 1)
                V.tensor_copy(xq[:, bass.ds(q, 1), 0, :, :].rearrange("p q c t -> p (q c t)"),
                              xi.rearrange("p c n t -> p (c n t)")).then_inc(S["xhi_done"], 1)
                dve.wait_ge(S["xhi_done"], q + 1)
                V.tensor_tensor(xq[:, bass.ds(q, 1), 1, :, :].rearrange("p q c t -> p (q c t)"),
                                xi.rearrange("p c n t -> p (c n t)"),
                                xq[:, bass.ds(q, 1), 0, :, :].rearrange("p q c t -> p (q c t)"),
                                ALU.subtract).then_inc(S["xlo_done"], 1)

            dve.wait_ge(S["xnt_out"], PAIRS)
            round_x(0)

            def largest(q, m):
                for f in range(FC):
                    dve.wait_ge(S["b_gelu"], q * FC + (f + 1 + FC))
                    V.tensor_reduce(hmax[:, bass.ds(q, 1), f], halls[m][:, f, :], AX_X, ALU.max,
                                    apply_absolute_value=True).then_inc(S["b_max"], 1)

            with dve.Fori(0, QUADS // 2 - 1) as i:
                round_x(i * 2 + 1)
                largest(i * 2, 0)
                round_x(i * 2 + 2)
                largest(i * 2 + 1, 1)
            round_x(QUADS - 1)
            largest(QUADS - 2, 0)
            largest(QUADS - 1, 1)
            for m in range(2):
                dve.wait_ge(s_h_st[m], 16 * (QUADS // 2))
            dve.wait_ge(S["b_max"], QUADS * FC)
            V.tensor_reduce(hm_part, hmax[:, :, :], AX_XY, ALU.max).then_inc(S["hmax_part"], 1)
            dve.wait_ge(S["hmax_all"], 1)
            then(V.tensor_scalar(h_amax, h_amax, TINY, None, ALU.max))
            then(V.reciprocal(h_up, h_amax))
            then(V.tensor_scalar(y_scale, h_amax, wo_top, 1.0 / INT8, ALU.mult, ALU.mult))
            then(V.tensor_scalar(y_scale, y_scale, 1.0 / INT16, None, ALU.mult))
            V.tensor_scalar(h_up, h_up, INT16, None, ALU.mult).then_inc(S["h_scale"], 1)
            dve.wait_ge(S["h_scale"], 1)

            def round_h(q, m, has_output=True):
                def high(f):
                    dve.wait_ge(S["c_hq"], q * FC + (f + 1))
                    if f == 0:
                        wait(dve, S["c_y"], (q - 1) * 4)
                    V.tensor_scalar(gbuf[m][:, 0, f, :], hq[f % 4], wout_rel[:, f:f + 1], None, ALU.mult).then_inc(S["c_hi"], 1)

                def rest(f):
                    dve.wait_ge(S["c_hi"], q * FC + (f + 1))
                    V.scalar_tensor_tensor(gbuf[m][:, 1, f, :], hq[f % 4], wout_rel[:, f:f + 1], gbuf[m][:, 0, f, :],
                                           ALU.mult, ALU.subtract).then_inc(S["c_lo"], 1)

                high(0)
                for f in range(1, FC):
                    high(f)
                    rest(f - 1)
                    if has_output and f >= FINISH_AT and f - FINISH_AT < 3:
                        finish(q - 1, 1 - m, f - FINISH_AT)
                rest(FC - 1)
                if has_output:
                    finish(q - 1, 1 - m, 3)

            def finish(q, m, k):
                if k == 0:
                    dve.wait_ge(S["c_x1b"], q + 1)
                dve.wait_ge(S["c_y"], q * 4 + (k + 1))
                V.scalar_tensor_tensor(yq[:, m, k, :], bank[4 + k][:, 0:D], y_scale, yq[:, m, k, :],
                                       ALU.mult, ALU.add).then_inc(S["c_out"], 1)

            round_h(0, 0, False)
            round_h(1, 1)
            with dve.Fori(1, QUADS // 2) as i:
                round_h(i * 2, 0)
                round_h(i * 2 + 1, 1)
            for k in range(4):
                finish(QUADS - 1, 1, k)


_INS = ["x", "ctx_1024", "ctx_turned", "L0_xattn_wq", "L0_xattn_wk", "L0_xattn_wv", "L0_xattn_wo",
        "L0_ffn_W_in", "L0_ffn_b_in", "L0_ffn_W_out", "L0_ffn_b_out"]


def kernel(**inputs):
    import numpy as _np
    import concourse.bacc as _bacc
    from concourse import mybir as _mybir
    from concourse.bass_utils import run_bass_kernel_spmd as _run

    nc = _bacc.Bacc("TRN2", target_bir_lowering=False, num_devices=1)
    arrays, args = {}, []
    c = _np.asarray(inputs["ctx_1024"])
    turned = c.reshape(c.shape[0] // 2, 2, P, 2, P).transpose(0, 4, 3, 1, 2).reshape(-1, P, 2, 2 * P)
    inputs = dict(inputs, ctx_turned=turned)
    for name in _INS:
        a = _np.asarray(inputs[name])
        if name.endswith("W_in"):
            a = a.T
        if name[-2:] in ("wq", "wk", "wv"):
            a = a.reshape(2 * P, NH, 2, HD).transpose(0, 2, 3, 1).reshape(a.shape)
        a = _np.ascontiguousarray(a)
        arrays[f"in_{name}"] = a
        args.append(nc.dram_tensor(f"in_{name}", a.shape, _mybir.dt.from_np(a.dtype), kind="ExternalInput").ap())
    for name, table in zip(("table", "inverse_table"), constants()):
        arrays[name] = table
        args.append(nc.dram_tensor(name, table.shape, _mybir.dt.from_np(table.dtype), kind="ExternalInput").ap())
    shape = inputs["x"].shape
    args.append(nc.dram_tensor("out_0", shape, _mybir.dt.float32, kind="ExternalOutput").ap())
    args.append(nc.dram_tensor("x1_scratch", shape, _mybir.dt.float32, kind="Internal").ap())
    args.append(nc.dram_tensor("hidden_scratch", (shape[0] // 4, P, SAVED * 4 * P), _mybir.dt.float32, kind="Internal").ap())
    xattn_ffn_kernel(nc, *args)
    return _run(nc, [arrays], core_ids=[0]).results[0]["out_0"]
```
